# Optimizing a Trainium2 kernel written in Bass

```python
import numpy as np
import jax
import jax.numpy as jnp

def _softmax(x, axis=-1):
    return jax.nn.softmax(x, axis=axis)

def _gelu(x):
    return jax.nn.gelu(x, approximate=True)

def _silu(x):
    return jax.nn.silu(x)

def _sigmoid(x):
    return jax.nn.sigmoid(x)

def _layernorm(x, axis=-1, eps=1e-05):
    m = jnp.mean(x, axis=axis, keepdims=True)
    v = jnp.var(x, axis=axis, keepdims=True)
    return (x - m) / jnp.sqrt(v + eps)

def _scatter_add(tgt, idx, src, axis=0):
    return tgt.at[idx].add(src)

def _segment_sum(src, seg, n):
    return jax.ops.segment_sum(src, seg, n)
kernel_name = 'mk_gnn_resnorm_d1_gnn_r32_e07ed5'

def setup_inputs(seed: int=0):
    np.random.seed(seed)
    _w = jnp.asarray

    def _rec_inputs():
        import jax
        import jax.numpy as jnp
        _gk = jax.random.key(seed)
        x = -0.0003713 + 1 * jax.random.normal(jax.random.fold_in(_gk, 1), (50000, 256), jnp.float32)
        _s = jax.random.randint(jax.random.fold_in(_gk, 2), (12500,), 0, 50000, jnp.int32)
        _d = jax.random.randint(jax.random.fold_in(_gk, 3), (12500,), 0, 50000, jnp.int32)
        _loop = jnp.arange(50000, dtype=jnp.int32)
        src = jnp.concatenate([_s, _d, _loop])
        dst = jnp.concatenate([_d, _s, _loop])
        _o = jnp.argsort(dst, stable=True)
        src = src[_o]
        dst = dst[_o]
        return (x, src, dst)
    x, src, dst = _rec_inputs()

    def _L0_gnn_setup():
        import jax, jax.numpy as jnp
        import numpy as np
        N = 50000
        E = 15625
        D = 256
        key = jax.random.key(seed)
        ks = jax.random.split(key, 12)
        s = 0.02
        x = jax.random.normal(ks[0], (N, D), dtype=jnp.float32)
        edge_index = jax.random.randint(ks[1], (2, E), 0, N, dtype=jnp.int64)
        W1 = jax.random.normal(ks[2], (D, 2 * D), dtype=jnp.float32) * s
        b1 = jax.random.normal(ks[3], (D,), dtype=jnp.float32) * s
        W2 = jax.random.normal(ks[4], (D, D), dtype=jnp.float32) * s
        b2 = jax.random.normal(ks[5], (D,), dtype=jnp.float32) * s
        w_ih = jax.random.normal(ks[6], (3 * D, D), dtype=jnp.float32) * s
        w_hh = jax.random.normal(ks[7], (3 * D, D), dtype=jnp.float32) * s
        b_ih = jax.random.normal(ks[8], (3 * D,), dtype=jnp.float32) * s
        b_hh = jax.random.normal(ks[9], (3 * D,), dtype=jnp.float32) * s
        gamma = jnp.ones((D,), dtype=jnp.float32)
        beta = jnp.zeros((D,), dtype=jnp.float32)
        return {'x': x, 'edge_index': edge_index, 'W1': W1, 'b1': b1, 'W2': W2, 'b2': b2, 'w_ih': w_ih, 'w_hh': w_hh, 'b_ih': b_ih, 'b_hh': b_hh, 'gamma': gamma, 'beta': beta}
    _L0_gnn_all = _L0_gnn_setup()
    _L0_gnn_in = {k: v for k, v in _L0_gnn_all.items() if k in ('W1', 'b1', 'W2', 'b2', 'w_ih', 'w_hh', 'b_ih', 'b_hh', 'gamma', 'beta')}
    del _L0_gnn_all
    return {'x': x, 'src': src, 'dst': dst, 'L0_gnn_W1': _L0_gnn_in['W1'], 'L0_gnn_b1': _L0_gnn_in['b1'], 'L0_gnn_W2': _L0_gnn_in['W2'], 'L0_gnn_b2': _L0_gnn_in['b2'], 'L0_gnn_w_ih': _L0_gnn_in['w_ih'], 'L0_gnn_w_hh': _L0_gnn_in['w_hh'], 'L0_gnn_b_ih': _L0_gnn_in['b_ih'], 'L0_gnn_b_hh': _L0_gnn_in['b_hh'], 'L0_gnn_gamma': _L0_gnn_in['gamma'], 'L0_gnn_beta': _L0_gnn_in['beta']}

def reference(x, src, dst, L0_gnn_W1, L0_gnn_b1, L0_gnn_W2, L0_gnn_b2, L0_gnn_w_ih, L0_gnn_w_hh, L0_gnn_b_ih, L0_gnn_b_hh, L0_gnn_gamma, L0_gnn_beta):
    import jax
    import jax.numpy as jnp

    def _L0_gnn_ref(x, edge_index, W1, b1, W2, b2, w_ih, w_hh, b_ih, b_hh, gamma, beta):
        import jax, jax.numpy as jnp
        import numpy as np
        N = 50000
        E = 15625
        D = 256
        n_nodes = x.shape[0]
        row, col = (edge_index[0], edge_index[1])
        h = jnp.concatenate([x[row], x[col]], axis=-1)
        msgs = jax.nn.silu(h @ W1.T + b1) @ W2.T + b2
        agg = jax.ops.segment_sum(msgs, row, num_segments=n_nodes)
        cnt = jax.ops.segment_sum(jnp.ones((row.shape[0], 1), x.dtype), row, num_segments=n_nodes)
        agg = agg / (cnt + 1e-08)
        gi = agg @ w_ih.T + b_ih
        gh = x @ w_hh.T + b_hh
        i_r, i_z, i_n = jnp.split(gi, 3, axis=-1)
        h_r, h_z, h_n = jnp.split(gh, 3, axis=-1)
        r = jax.nn.sigmoid(i_r + h_r)
        z = jax.nn.sigmoid(i_z + h_z)
        n = jnp.tanh(i_n + r * h_n)
        x_new = (1.0 - z) * n + z * x
        mu = jnp.mean(x_new, axis=-1, keepdims=True)
        var = jnp.var(x_new, axis=-1, keepdims=True)
        return gamma * (x_new - mu) / jnp.sqrt(var + 1e-05) + beta
    edge_index = jnp.stack([src, dst])
    x = _layernorm(x + _L0_gnn_ref(x, edge_index, L0_gnn_W1, L0_gnn_b1, L0_gnn_W2, L0_gnn_b2, L0_gnn_w_ih, L0_gnn_w_hh, L0_gnn_b_ih, L0_gnn_b_hh, L0_gnn_gamma, L0_gnn_beta), axis=-1)
    return x

_drawn_inputs = setup_inputs


def setup_inputs(seed=0):
    import zlib

    import numpy as np

    out = dict(_drawn_inputs(seed))
    spreads = {'L0_gnn_gamma': (1.0, 0.2), 'L0_gnn_beta': (0.0, 0.1)}
    factors = {'L0_gnn_W1': 4.602,
     'L0_gnn_b1': 8.0,
     'L0_gnn_W2': 4.462,
     'L0_gnn_b2': 8.0,
     'L0_gnn_w_ih': 4.324,
     'L0_gnn_b_ih': 5.352,
     'L0_gnn_b_hh': 8.0}
    for name, (base, spread) in spreads.items():
        noise = np.random.default_rng([zlib.crc32(name.encode()), seed]).standard_normal(out[name].shape)
        drawn = base * np.exp(spread * noise) if base else spread * noise
        out[name] = jnp.asarray(drawn.astype(out[name].dtype))
    for name, factor in factors.items():
        out[name] = (out[name] * factor).astype(out[name].dtype)
    return out
```

```python
from contextlib import ExitStack

import concourse.bass as bass
from concourse import mybir

F32 = mybir.dt.float32
F32R = mybir.dt.float32r
F16 = mybir.dt.float16
I32 = mybir.dt.int32
ALU = mybir.AluOpType
ACT = mybir.ActivationFunctionType
AX = mybir.AxisListType

P = 128
N, D = 50000, 256
E = 75000
NT = -(-N // P)
LAST_ROWS = N - (NT - 1) * P
KC = D // P
EC = -(-E // P)
ES = 9
TW = 1 << ES
ROUND = P * TW
FAST = 2
ROUNDS = -(-E // P)
EMPTY = 255 << 16
NW = NT + 1
PAIRS = EC // 2
MT, MP = 4, 3
MACROS = -(-NT // MT)
LAST_MT = NT - (MACROS - 1) * MT
LAST_MP = PAIRS - (MACROS - 1) * MP
TAIL = N - (MACROS - 1) * MT * P
TAIL_P = TAIL // LAST_MT
assert TAIL_P * LAST_MT == TAIL and EC == 2 * PAIRS and 0 < LAST_MP <= MP
XS = 6
LO = 8
LOOPS = (NT - 1 - 4 - LO) // XS
HI = LO + XS * LOOPS
EPS = 1e-5


def build(nc, x, src, dst, W1, b1, W2, b2, w_ih, w_hh, b_ih, b_hh, gamma, beta, out):
    ctx = ExitStack()
    with ctx:
        def sb(name, shape, dt):
            return ctx.enter_context(nc.sbuf_tensor("sb_" + name, shape, dt))

        def sem(name):
            return ctx.enter_context(nc.semaphore(name))

        xb_rows = nc.dram_tensor("xb_rows", [N, D], F32, kind="Internal").ap()
        table = nc.dram_tensor("edge_table", [ROUNDS * ROUND, 1], I32, kind="Internal").ap()

        banks = [ctx.enter_context(nc.psum_tensor(f"bank{n}", [P, 512], F32)) for n in range(8)]

        ident = sb("ident", [P, P], F32)
        lane = sb("lane", [P, P], F32)
        gamma_b = sb("gamma_b", [P, D], F32)
        beta_b = sb("beta_b", [P, D], F32)
        w1a = [sb(f"w1a{n}", [P, KC, D], F32R) for n in range(2)]
        w1b = [sb(f"w1b{n}", [P, KC, D], F32R) for n in range(2)]
        whh = [sb(f"whh{n}", [P, KC, 3 * D], F32R) for n in range(2)]
        wc = [sb(f"wc{n}", [P, KC, 3 * D], F32R) for n in range(2)]
        gi_bias = sb("gi_bias", [4, 3 * D], F32R)
        hn_bias = sb("hn_bias", [2, D], F32R)
        b1_bias = sb("b1_bias", [2, D], F32R)
        ones2 = sb("ones2", [2, P], F32R)
        columns = sb("columns", [P, 3], F32)
        slots = sb("slots", [P, 2 * FAST, TW], I32)
        index_all = sb("index_all", [P, EC + 2], I32)
        pay_all = sb("pay_all", [P, EC + 2], I32)
        rounds_i = sb("rounds_i", [P, 1], I32)

        const_made = sem("const_made")
        weights_loaded = sem("weights_loaded")
        w_transposed = sem("w_transposed")
        w_high = sem("w_high")
        w_evac = sem("w_evac")
        rows_ready = sem("rows_ready")
        rows_high = sem("rows_high")
        rows_low = sem("rows_low")
        rows_placed = sem("rows_placed")
        edges_loaded = sem("edges_loaded")
        edges_ready = sem("edges_ready")
        empty_made = sem("empty_made")
        table_cleared = sem("table_cleared")
        with ExitStack() as tmp:
            def tb(name, shape, dt):
                return tmp.enter_context(nc.sbuf_tensor("sb_" + name, shape, dt))

            w1_raw = tb("w1_raw", [P, 2, 2 * D], F32)
            whh_raw = tb("whh_raw", [P, 6, D], F32)
            wih_raw = tb("wih_raw", [P, 6, D], F32)
            w2_raw = tb("w2_raw", [P, 2, D], F32)
            wih_t = tb("wih_t", [P, KC, 3 * D], F32)
            b2_col = tb("b2_col", [P, KC], F32)
            bi_row = tb("bi_row", [1, 3 * D], F32)
            bh_row = tb("bh_row", [1, 3 * D], F32)
            b1_row = tb("b1_row", [1, D], F32)
            c_row = tb("c_row", [1, 5 * D], F32)
            c_high = tb("c_high", [1, 5 * D], F32R)
            c_low = tb("c_low", [1, 5 * D], F32R)
            b2w_high = tb("b2w_high", [1, 3 * D], F32R)
            b2w_low = tb("b2w_low", [1, 3 * D], F32R)
            ones_f = tb("ones_f", [2, P], F32)
            empty = tb("empty", [P, FAST * ROUND // P], I32)

            banks_of = []
            for raw, chunk, target, width in ((w1_raw, 0, w1a, D), (w1_raw, D, w1b, D),
                                              (whh_raw, 0, whh, 3 * D), (wih_raw, 0, None, 3 * D)):
                blocks = [(raw, o, chunk + k * P) for k in range(KC) for o in range(width // P)]
                for n in range(0, len(blocks), 4):
                    banks_of.append((target, n * P, blocks[n:n + 4]))
            n_t = len(banks_of)
            pieces = [(k, c) for k in range(KC) for c in range(3)]
            flat = lambda t: t[:, :, :].rearrange("p k n -> p (k n)")

            with nc.Block() as block:
                @block.sync
                def _(sp):
                    sp.dma_start(w1_raw[:, :, :], W1.rearrange("(o p) k -> p o k", p=P)).then_inc(weights_loaded, 16)
                    sp.dma_start(whh_raw[:, :, :], w_hh.rearrange("(o p) k -> p o k", p=P)).then_inc(weights_loaded, 16)
                    sp.dma_start(wih_raw[:, :, :], w_ih.rearrange("(o p) k -> p o k", p=P)).then_inc(weights_loaded, 16)
                    sp.dma_start(w2_raw[:, :, :], W2.rearrange("(o p) k -> p o k", p=P)).then_inc(weights_loaded, 16)
                    with nc.allow_non_contiguous_dma(reason="256 values, once"):
                        sp.dma_start(b2_col[:, :], b2.rearrange("(c p) -> p c", p=P)).then_inc(weights_loaded, 16)
                    sp.dma_start(bi_row[:, :], b_ih.rearrange("(a n) -> a n", a=1)).then_inc(weights_loaded, 16)
                    sp.dma_start(bh_row[:, :], b_hh.rearrange("(a n) -> a n", a=1)).then_inc(weights_loaded, 16)
                    sp.dma_start(b1_row[:, :], b1.rearrange("(a n) -> a n", a=1)).then_inc(weights_loaded, 16)
                    for row, wide in ((gamma, gamma_b), (beta, beta_b)):
                        sp.dma_start(wide[:, :], row.rearrange("(a n) -> a n", a=1).to_broadcast([P, D])).then_inc(weights_loaded, 16)
                    sp.wait_ge(empty_made, 1)
                    sp.dma_start(table[0:FAST * ROUND, :].rearrange("(p n) a -> p (n a)", p=P), empty[:, :]).then_inc(table_cleared, 16)
                    sp.wait_ge(rows_low, 2)
                    sp.dma_start(gi_bias[0:1, :].bitcast(F32), b2w_high[:, :].bitcast(F32)).then_inc(rows_placed, 16)
                    sp.dma_start(gi_bias[1:2, :].bitcast(F32), b2w_low[:, :].bitcast(F32)).then_inc(rows_placed, 16)
                    sp.dma_start(gi_bias[2:3, :].bitcast(F32), c_high[:, 0:3 * D].bitcast(F32)).then_inc(rows_placed, 16)
                    sp.dma_start(gi_bias[3:4, :].bitcast(F32), c_low[:, 0:3 * D].bitcast(F32)).then_inc(rows_placed, 16)
                    sp.dma_start(hn_bias[0:1, :].bitcast(F32), c_high[:, 3 * D:4 * D].bitcast(F32)).then_inc(rows_placed, 16)
                    sp.dma_start(hn_bias[1:2, :].bitcast(F32), c_low[:, 3 * D:4 * D].bitcast(F32)).then_inc(rows_placed, 16)
                    sp.dma_start(b1_bias[0:1, :].bitcast(F32), c_high[:, 4 * D:5 * D].bitcast(F32)).then_inc(rows_placed, 16)
                    sp.dma_start(b1_bias[1:2, :].bitcast(F32), c_low[:, 4 * D:5 * D].bitcast(F32)).then_inc(rows_placed, 16)
                    sp.wait_ge(rows_placed, 128)
                    sp.wait_ge(table_cleared, 16)

                @block.gpsimd
                def _(pool):
                    nc.gpsimd.memset(ident[:, :], 0.0).then_inc(const_made, 1)
                    pool.wait_ge(const_made, 1)
                    nc.gpsimd.affine_select(out=ident[:, :], in_=ident[:, :], compare_op=ALU.not_equal, fill=1.0,
                                            base=0, pattern=[[-1, P]], channel_multiplier=1).then_inc(const_made, 1)
                    nc.gpsimd.iota(lane[:, :], [[1, P]], base=0, channel_multiplier=0,
                                   allow_small_or_imprecise_dtypes=True).then_inc(const_made, 1)
                    nc.gpsimd.memset(columns[:, 0:1], -0.5)
                    nc.gpsimd.memset(columns[:, 1:2], EPS)
                    nc.gpsimd.memset(columns[:, 2:3], -1.0).then_inc(const_made, 1)

                @block.tensor
                def _(pe):
                    pe.wait_ge(weights_loaded, 160)
                    pe.wait_ge(const_made, 2)
                    for n, (_, _, blocks) in enumerate(banks_of):
                        if n >= 8:
                            pe.wait_ge(w_evac, n - 7)
                        for b, (raw, o, col) in enumerate(blocks):
                            last = nc.tensor.transpose(banks[n % 8][:, b * P:(b + 1) * P], raw[:, o, col:col + P], ident[:, :])
                        last.then_inc(w_transposed, 1)
                    pe.wait_ge(w_evac, n_t)
                    for n in range(3):
                        m = n_t + n
                        for half in range(2):
                            k, c = pieces[2 * n + half]
                            for d in range(KC):
                                last = nc.tensor.matmul(banks[m % 8][:, half * D:(half + 1) * D], w2_raw[:, d, k * P:(k + 1) * P],
                                                        wih_t[:, d, c * D:(c + 1) * D], start=(d == 0), stop=(d == KC - 1))
                        last.then_inc(w_transposed, 1)
                    for n, (a, z) in enumerate(((0, 2 * D), (2 * D, 3 * D))):
                        m = n_t + 3 + n
                        for d in range(KC):
                            last = nc.tensor.matmul(banks[m % 8][0:1, 0:z - a], b2_col[:, d:d + 1], wih_t[:, d, a:z],
                                                    start=(d == 0), stop=(d == KC - 1))
                        last.then_inc(w_transposed, 1)

                @block.scalar
                def _(act):
                    for n, (target, col, _) in enumerate(banks_of):
                        if target is not None:
                            act.wait_ge(w_transposed, n + 1)
                            nc.scalar.activation(flat(target[0])[:, col:col + 512], banks[n % 8][:, :], ACT.Copy).then_inc(w_high, 1)
                    for n in range(3):
                        act.wait_ge(w_transposed, n_t + n + 1)
                        nc.scalar.activation(flat(wc[0])[:, n * 512:(n + 1) * 512], banks[(n_t + n) % 8][:, :], ACT.Copy).then_inc(w_high, 1)
                    for n, (a, z) in enumerate(((0, 2 * D), (2 * D, 3 * D))):
                        act.wait_ge(w_transposed, n_t + 4 + n)
                        nc.scalar.activation(b2w_high[:, a:z], banks[(n_t + 3 + n) % 8][0:1, 0:z - a], ACT.Copy).then_inc(w_high, 1)
                    act.wait_ge(rows_ready, 3)
                    nc.scalar.activation(c_high[:, :], c_row[:, :], ACT.Copy).then_inc(rows_high, 1)

                @block.vector
                def _(dve):
                    nc.vector.memset(empty[:, :], EMPTY).then_inc(empty_made, 1)
                    nc.vector.memset(ones_f[:, :], 1.0).then_inc(rows_ready, 1)
                    dve.wait_ge(weights_loaded, 160)
                    nc.vector.tensor_tensor(c_row[:, 0:2 * D], bi_row[:, 0:2 * D], bh_row[:, 0:2 * D], ALU.add).then_inc(rows_ready, 1)
                    nc.vector.tensor_copy(c_row[:, 2 * D:3 * D], bi_row[:, 2 * D:3 * D])
                    nc.vector.tensor_copy(c_row[:, 4 * D:5 * D], b1_row[:, :])
                    nc.vector.tensor_copy(c_row[:, 3 * D:4 * D], bh_row[:, 2 * D:3 * D]).then_inc(rows_ready, 1)
                    dve.wait_ge(rows_ready, 1)
                    nc.vector.tensor_copy(ones2[:, :], ones_f[:, :])
                    high = 0
                    for n, (target, col, _) in enumerate(banks_of):
                        dve.wait_ge(w_transposed, n + 1)
                        if target is None:
                            nc.vector.tensor_copy(flat(wih_t)[:, col:col + 512], banks[n % 8][:, :]).then_inc(w_evac, 1)
                        else:
                            high += 1
                            dve.wait_ge(w_high, high)
                            nc.vector.tensor_tensor(flat(target[1])[:, col:col + 512], banks[n % 8][:, :],
                                                    flat(target[0])[:, col:col + 512], ALU.subtract).then_inc(w_evac, 1)
                    for n in range(3):
                        high += 1
                        dve.wait_ge(w_high, high)
                        nc.vector.tensor_tensor(flat(wc[1])[:, n * 512:(n + 1) * 512], banks[(n_t + n) % 8][:, :],
                                                flat(wc[0])[:, n * 512:(n + 1) * 512], ALU.subtract).then_inc(w_evac, 1)
                    for n, (a, z) in enumerate(((0, 2 * D), (2 * D, 3 * D))):
                        high += 1
                        dve.wait_ge(w_high, high)
                        last = nc.vector.tensor_tensor(b2w_low[:, a:z], banks[(n_t + 3 + n) % 8][0:1, 0:z - a],
                                                       b2w_high[:, a:z], ALU.subtract)
                    last.then_inc(rows_low, 1)
                    dve.wait_ge(rows_high, 1)
                    nc.vector.tensor_tensor(c_low[:, :], c_row[:, :], c_high[:, :], ALU.subtract).then_inc(rows_low, 1)

        tri_made = sem("tri_made")
        x_in = [sem(f"x_in{n}") for n in range(2)]
        xt2_done = sem("xt2_done")
        high2_done = sem("high2_done")
        low2_done = sem("low2_done")
        rowmm_done = sem("rowmm_done")
        row_evac = sem("row_evac")
        row_stored = [sem(f"row_stored{n}") for n in range(2)]
        onehot_ready = sem("onehot_ready")
        rank_mm = [sem(f"rank_mm{n}") for n in range(2)]
        rank_read = [sem(f"rank_read{n}") for n in range(2)]
        rank_int = sem("rank_int")
        index_ready = sem("index_ready")
        index_copied = sem("index_copied")
        index_kept = sem("index_kept")
        scattered = [sem(f"scattered{n}") for n in range(2)]
        counts_done = sem("counts_done")
        rounds_done = sem("rounds_done")
        with ExitStack() as tmp:
            def tb(name, shape, dt):
                return tmp.enter_context(nc.sbuf_tensor("sb_" + name, shape, dt))

            src_i = tb("src_i", [P, EC], I32)
            dst_i = tb("dst_i", [P, EC], I32)
            tile_i = tb("tile_i", [P, EC + 2], I32)
            tile_f = tb("tile_f", [P, EC + 2], F32)
            tiles16 = tb("tiles16", [P, NW], F16)
            tri = tb("tri", [P, P], F16)
            rest = tb("rest", [P, P], F16)
            ones16 = tb("ones16", [P, P], F16)
            onehot = tb("onehot", [P, 3, 2, NW], F16)
            scratch = tb("scratch", [P, 2, NW], F16)
            rank = tb("rank", [P, 2, 2 * MP], F32)
            rank_i = tb("rank_i", [P, 2, 2 * MP], I32)
            index = tb("index", [P, 2, 2 * MP], I32)
            pay = tb("pay", [P, 2, 2 * MP], I32)
            rounds_f = tb("rounds_f", [P, 1], F32)
            rounds_t = tb("rounds_t", [P, 1], I32)
            x2 = tb("x2", [P, 2, MT, D], F32)
            xt_high = tb("xt_high", [P, 2, KC, P], F32R)
            xt_low = tb("xt_low", [P, 2, KC, P], F32R)
            rows = tb("rows", [P, 2, MT, D], F32)
            FULL = E // EC
            REST = E - FULL * EC

            rank_bank = banks[0:2]
            xt_bank = banks[2:4]
            row_bank = banks[4:6]
            prep = sem("prep")

            with nc.Block() as block:
                @block.sync
                def _(sp):
                    sp.wait_ge(tri_made, 1)
                    sp.dma_start(src_i[0:FULL, :], src[0:FULL * EC].rearrange("(p c) -> p c", c=EC)).then_inc(edges_loaded, 16)
                    sp.dma_start(dst_i[0:FULL, :], dst[0:FULL * EC].rearrange("(p c) -> p c", c=EC)).then_inc(edges_loaded, 16)
                    sp.dma_start(src_i[FULL:P, 0:REST], src[FULL * EC:E].rearrange("(p c) -> p c", p=1)).then_inc(edges_loaded, 16)
                    sp.dma_start(dst_i[FULL:P, 0:REST], dst[FULL * EC:E].rearrange("(p c) -> p c", p=1)).then_inc(edges_loaded, 16)

                @block.gpsimd
                def _(pool):
                    nc.gpsimd.iota(src_i[:, :], [[P, EC]], base=(NW + 8 - REST) * P, channel_multiplier=0)
                    nc.gpsimd.memset(dst_i[:, :], 0).then_inc(tri_made, 1)
                    nc.gpsimd.iota(tiles16[:, :], [[1, NW]], base=0, channel_multiplier=0,
                                   allow_small_or_imprecise_dtypes=True).then_inc(tri_made, 1)
                    nc.gpsimd.memset(tri[:, :], 1.0)
                    nc.gpsimd.memset(rest[:, :], 1.0)
                    nc.gpsimd.memset(ones16[:, :], 1.0).then_inc(tri_made, 1)
                    pool.wait_ge(tri_made, 3)
                    nc.gpsimd.affine_select(out=tri[:, :], in_=tri[:, :], compare_op=ALU.is_gt, fill=0.0,
                                            base=0, pattern=[[1, P]], channel_multiplier=-1)
                    nc.gpsimd.affine_select(out=rest[:, :], in_=rest[:, :], compare_op=ALU.is_ge, fill=0.0,
                                            base=0, pattern=[[-1, P]], channel_multiplier=1).then_inc(tri_made, 1)

                @block.vector
                def _(dve):
                    dve.wait_ge(edges_loaded, 64)
                    dve.wait_ge(tri_made, 4)
                    nc.vector.memset(tile_i[:, EC:EC + 2], 0)
                    nc.vector.tensor_scalar(tile_i[:, 0:EC], src_i[:, :], 7, None, ALU.logical_shift_right).then_inc(prep, 1)
                    dve.wait_ge(prep, 1)
                    nc.vector.tensor_copy(tile_f[:, :], tile_i[:, :])
                    nc.vector.tensor_scalar(pay_all[:, 0:EC], src_i[:, :], P - 1, 16, ALU.bitwise_and,
                                            ALU.logical_shift_left).then_inc(prep, 1)
                    dve.wait_ge(prep, 2)
                    nc.vector.tensor_tensor(pay_all[:, 0:EC], pay_all[:, 0:EC], dst_i[:, :], ALU.bitwise_or).then_inc(prep, 1)
                    nc.vector.memset(pay_all[:, EC:EC + 2], 0)
                    nc.vector.memset(index_all[:, :], 0)
                    nc.vector.memset(x2[:, :, :, :], 0.0).then_inc(prep, 1)

            def macro_steps(eng, step):
                for c in range(3):
                    step(0, c)
                with eng.Fori(0, (MACROS - 4) // 2) as u:
                    for c in (3, 4):
                        step(u, c)
                step(0, MACROS - 1)

            def tiles_of(c):
                return LAST_MT if c == MACROS - 1 else MT

            def pairs_of(c):
                return LAST_MP if c == MACROS - 1 else MP

            def node_rows(t, u, c):
                if c == MACROS - 1:
                    return t[c * MT * P:N, :].rearrange("(p q) d -> p q d", q=LAST_MT), TAIL_P, LAST_MT
                return t[bass.ds((2 * u + c) * (MT * P), MT * P), :].rearrange("(p q) d -> p q d", q=MT), P, MT

            with nc.Block() as block:
                @block.sync
                def _(sp):
                    def store(u, c):
                        rows_out, np_, nq = node_rows(xb_rows, u, c)
                        sp.wait_ge(row_evac, 2 * MT * u + (MT * c + tiles_of(c)))
                        sp.dma_start(rows_out, rows[0:np_, c % 2, 0:nq, :]).then_inc(row_stored[c % 2], 16)

                    def step(u, c):
                        rows_in, np_, nq = node_rows(x, u, c)
                        if c >= 2:
                            sp.wait_ge(xt2_done, 2 * MT * u + MT * (c - 1))
                        sp.dma_start(x2[0:np_, c % 2, 0:nq, :], rows_in).then_inc(x_in[c % 2], 16)
                        if c >= 2:
                            store(u, c - 2)

                    macro_steps(sp, step)
                    store(0, MACROS - 2)
                    store(0, MACROS - 1)
                    sp.wait_ge(row_stored[0], 16 * ((MACROS + 1) // 2))
                    sp.wait_ge(row_stored[1], 16 * (MACROS // 2))

                @block.tensor
                def _(pe):
                    def transposes(u, c, q):
                        if q == 0:
                            pe.wait_ge(x_in[c % 2], 16 * u + 16 * (c // 2 + 1))
                        k = MT * c + q
                        if k >= 2:
                            pe.wait_ge(low2_done, 2 * MT * u + (k - 1))
                        for d in range(KC):
                            last = nc.tensor.transpose(xt_bank[q % 2][:, d * P:(d + 1) * P], x2[:, c % 2, q, d * P:(d + 1) * P], ident[:, :])
                        last.then_inc(xt2_done, 1)

                    def product(u, c, q):
                        k = MT * c + q
                        pe.wait_ge(low2_done, 2 * MT * u + (k + 1))
                        if k >= 2:
                            pe.wait_ge(row_evac, 2 * MT * u + (k - 1))
                        nc.tensor.matmul(row_bank[q % 2][:, 0:D], ones2[:, :], b1_bias[:, :], start=True, stop=False)
                        n = 0
                        for xt, w in ((xt_high, w1b[0]), (xt_high, w1b[1]), (xt_low, w1b[0])):
                            for d in range(KC):
                                last = nc.tensor.matmul(row_bank[q % 2][:, 0:D], xt[:, q % 2, d, :], w[:, d, :], start=False, stop=(n == 5))
                                n += 1
                        last.then_inc(rowmm_done, 1)

                    def count(bank, left, q, half, first=False, last=False):
                        return nc.tensor.matmul(rank_bank[bank][:, 0:NW], left[:, :], onehot[:, q % 3, half, :],
                                                start=first, stop=last, skip_group_check=True)

                    def ranks(u, c, q):
                        g = MP * c + q
                        first = g == 0
                        if not first:
                            pe.wait_ge(rank_read[0], 2 * MP * u + g)
                            count(0, rest, q - 1, 0)
                            count(0, ones16, q - 1, 1)
                        pe.wait_ge(onehot_ready, 2 * MP * u + (g + 1))
                        count(0, tri, q, 0, first, True).then_inc(rank_mm[0], 1)
                        if not first:
                            pe.wait_ge(rank_read[1], 2 * MP * u + g)
                            count(1, rest, q - 1, 1)
                        count(1, ones16, q, 0, first)
                        count(1, tri, q, 1, False, True).then_inc(rank_mm[1], 1)

                    def step(u, c):
                        for q in range(tiles_of(c)):
                            transposes(u, c, q)
                            if q < pairs_of(c):
                                ranks(u, c, q)
                            if c or q:
                                if q:
                                    product(u, c, q - 1)
                                else:
                                    product(u, c - 1, MT - 1)

                    macro_steps(pe, step)
                    product(0, MACROS - 1, LAST_MT - 1)
                    pe.wait_ge(rank_read[0], PAIRS)
                    count(0, rest, LAST_MP - 1, 0)
                    count(0, ones16, LAST_MP - 1, 1, False, True).then_inc(counts_done, 1)

                @block.scalar
                def _(act):
                    def high(u, c, q):
                        k = MT * c + q
                        act.wait_ge(xt2_done, 2 * MT * u + (k + 1))
                        if k >= 2:
                            act.wait_ge(rowmm_done, 2 * MT * u + (k - 1))
                        nc.scalar.activation(xt_high[:, q % 2, :, :].rearrange("p k n -> p (k n)"), xt_bank[q % 2][:, 0:D], ACT.Copy).then_inc(high2_done, 1)

                    def evacuate(u, c, q):
                        k = MT * c + q
                        act.wait_ge(rowmm_done, 2 * MT * u + (k + 1))
                        if q == 0 and c >= 2:
                            act.wait_ge(row_stored[c % 2], 16 * u + 16 * (c // 2))
                        nc.scalar.activation(rows[:, c % 2, q, :], row_bank[q % 2][:, 0:D], ACT.Copy).then_inc(row_evac, 1)

                    def payload(u, c):
                        b = 2 * pairs_of(c)
                        if c >= 2:
                            act.wait_ge(scattered[c % 2], 32 * MP * u + 32 * MP * (c // 2))
                        nc.scalar.activation(pay[:, c % 2, 0:b], pay_all[:, bass.ds(4 * MP * u + 2 * MP * c, b)], ACT.Copy).then_inc(index_copied, 1)

                    def step(u, c):
                        for q in range(tiles_of(c)):
                            if q == 2:
                                payload(u, c)
                            high(u, c, q)
                            if c or q:
                                if q:
                                    evacuate(u, c, q - 1)
                                else:
                                    evacuate(u, c - 1, MT - 1)

                    macro_steps(act, step)
                    evacuate(0, MACROS - 1, LAST_MT - 1)

                @block.vector
                def _(dve):
                    def onehots(u, c, q):
                        g = MP * c + q
                        if g >= 3:
                            dve.wait_ge(rank_mm[1], 2 * MP * u + (g - 1))
                        for half in range(2):
                            last = nc.vector.tensor_scalar(onehot[:, q % 3, half, :], tiles16[:, :],
                                                           tile_f[:, bass.ds(4 * MP * u + (2 * g + half), 1)], None, ALU.is_equal)
                        last.then_inc(onehot_ready, 1)

                    def read_ranks(u, c, q):
                        g = MP * c + q
                        for half in range(2):
                            dve.wait_ge(rank_mm[half], 2 * MP * u + (g + 1))
                            nc.vector.tensor_tensor_reduce(out=scratch[:, half, :], in0=rank_bank[half][:, 0:NW], in1=onehot[:, q, half, :],
                                                           scale=1.0, scalar=0.0, op0=ALU.mult, op1=ALU.add,
                                                           accum_out=rank[:, c % 2, 2 * q + half:2 * q + half + 1]).then_inc(rank_read[half], 1)

                    def low(u, c, q):
                        k = MT * c + q
                        dve.wait_ge(high2_done, 2 * MT * u + (k + 1))
                        nc.vector.tensor_tensor(xt_low[:, q % 2, :, :].rearrange("p k n -> p (k n)"), xt_bank[q % 2][:, 0:D],
                                                xt_high[:, q % 2, :, :].rearrange("p k n -> p (k n)"), ALU.subtract).then_inc(low2_done, 1)

                    def indices(u, c):
                        b = 2 * pairs_of(c)
                        dve.wait_ge(rank_read[1], 2 * MP * u + (MP * c + pairs_of(c)))
                        nc.vector.tensor_copy(rank_i[:, c % 2, 0:b], rank[:, c % 2, 0:b]).then_inc(rank_int, 1)
                        dve.wait_ge(rank_int, 2 * u + (c + 1))
                        if c >= 2:
                            dve.wait_ge(scattered[c % 2], 32 * MP * u + 32 * MP * (c // 2))
                            dve.wait_ge(index_kept, 2 * u + (c - 1))
                        nc.vector.scalar_tensor_tensor(out=index[:, c % 2, 0:b], in0=rank_i[:, c % 2, 0:b], scalar=ES,
                                                       in1=tile_i[:, bass.ds(4 * MP * u + 2 * MP * c, b)],
                                                       op0=ALU.logical_shift_left, op1=ALU.bitwise_or).then_inc(index_ready, 1)

                    def step(u, c):
                        for q in range(tiles_of(c)):
                            if q < pairs_of(c):
                                if q + 1 < pairs_of(c):
                                    onehots(u, c, q + 1)
                                elif c + 1 < MACROS:
                                    onehots(u, c + 1, 0)
                            low(u, c, q)
                            if q < pairs_of(c):
                                read_ranks(u, c, q)
                            if q == pairs_of(c) - 1:
                                indices(u, c)

                    onehots(0, 0, 0)
                    macro_steps(dve, step)
                    dve.wait_ge(counts_done, 1)
                    nc.vector.reduce_max(rounds_f[:, :], rank_bank[0][:, 0:NW], AX.X).then_inc(rounds_done, 1)
                    dve.wait_ge(rounds_done, 1)
                    nc.vector.tensor_scalar(rounds_t[:, :], rounds_f[:, :], float(P - 1), None, ALU.add).then_inc(rounds_done, 1)
                    dve.wait_ge(rounds_done, 2)
                    nc.vector.tensor_scalar(rounds_i[:, :], rounds_t[:, :], 7, None, ALU.logical_shift_right).then_inc(rounds_done, 1)

                @block.gpsimd
                def _(pool):
                    last_entry = pool.to_reg(FAST * ROUND - 1)

                    def step(u, c):
                        b = 2 * pairs_of(c)
                        pool.wait_ge(index_ready, 2 * u + (c + 1))
                        pool.wait_ge(index_copied, 2 * u + (c + 1))
                        nc.gpsimd.tensor_copy(index_all[:, bass.ds(4 * MP * u + 2 * MP * c, b)], index[:, c % 2, 0:b]).then_inc(index_kept, 1)
                        for n in range(b):
                            pool.indirect_dma_start(table, bass.IndirectOffsetOnAxis(ap=index[:, c % 2, n:n + 1], axis=0),
                                                    pay[:, c % 2, n:n + 1], None, bounds_check=last_entry,
                                                    oob_is_err=False).then_inc(scattered[c % 2], 16)

                    macro_steps(pool, step)
                    pool.wait_ge(scattered[0], 32 * MP * (MACROS // 2))
                    pool.wait_ge(scattered[1], 32 * MP * (MACROS // 2 - 1) + 32 * LAST_MP)

        rounds_there = sem("rounds_there")
        free_made = sem("free_made")
        further_done = sem("further_done")
        again_copied = sem("again_copied")
        again_scattered = sem("again_scattered")
        m_free = sem("m_free")
        rounds = {}
        table_rows = table.rearrange("(q h) a -> q (h a)", h=TW)
        decoded = sem("decoded")
        fixed_made = sem("fixed_made")
        with ExitStack() as tmp:
            def tb(name, shape, dt):
                return tmp.enter_context(nc.sbuf_tensor("sb_" + name, shape, dt))

            xs = tb("xs", [P, XS, D], F32)
            slot = tb("slot", [P, 3, 2 * FAST], I32)
            got = tb("got", [P, 3, FAST * D], F32)
            sel = tb("sel", [P, 3, FAST, P], F32R)
            sel_t = tb("sel_t", [P, 3, FAST * P], F32R)
            xh = tb("xh", [P, 2, KC, P], F32R)
            xl = tb("xl", [P, 2, KC, P], F32R)
            ah = tb("ah", [P, 2, D], F32R)
            al = tb("al", [P, 2, D], F32R)
            pre = tb("pre", [P, 2, FAST * D], F32)
            msg = tb("msg", [P, FAST, D], F32)
            msg_h = tb("msg_h", [P, 2, FAST, D + 2], F32R)
            msg_l = tb("msg_l", [P, 2, FAST, D], F32R)
            inv = tb("inv", [P, 2, 2], F32)
            mean = tb("mean", [P, 2, 3 * P], F32)
            mh = tb("mh", [P, 2, 3 * P], F32R)
            ml = tb("ml", [P, 2, 2 * P], F32R)
            trz = tb("trz", [P, 2, 2 * D], F32)
            u_sb = tb("u_sb", [P, 2, D], F32)
            cand_in = tb("cand_in", [P, 2, D], F32)
            cand = tb("cand", [P, 2, D], F32)
            diff = tb("diff", [P, 2, D], F32)
            xbeta = tb("xbeta", [P, 3, D], F32)
            zd = tb("zd", [P, 2, D], F32)
            xn = tb("xn", [P, 3, D], F32)
            stats = tb("stats", [P, 2, 6], F32)
            mv = tb("mv", [P, 2, 3, 2], F32)
            shift = tb("shift", [P, 3], F32)
            arg = tb("arg", [P, 2, 3], F32)
            minus_mean = tb("minus_mean", [P, 3], F32)
            rstd = tb("rstd", [P, 2, 3], F32)
            g_sb = tb("g_sb", [P, 2, D], F32)
            o_sb = tb("o_sb", [P, 3, D], F32)
            out_sb = tb("out_sb", [P, 3, D], F32)
            raw = tb("raw", [P, FAST, TW], I32)
            lanes_i = tb("lanes_i", [P, FAST, TW], I32)

            free = tb("free", [P, TW], I32)
            spare = tb("spare", [P, 2], F32)
            spare_v = tb("spare_v", [P, 1], F32)
            again = tb("again", [P, 2, 2], I32)
            more_i = tb("more_i", [1, 2, NW], I32)
            more_f = tb("more_f", [1, 3, NW], F32)
            further_i = tb("further_i", [1, 2, NW], I32)
            m_raw = tb("m_raw", [P, 1], I32)
            m_dst = tb("m_dst", [P, 1], I32)
            m_lane_i = tb("m_lane_i", [P, 1], I32)
            m_lane = tb("m_lane", [P, 1], F32)
            m_sel = tb("m_sel", [P, P], F32R)
            m_sel_t = tb("m_sel_t", [P, P], F32R)
            m_got = tb("m_got", [P, D], F32)
            m_pre = tb("m_pre", [P, D], F32)
            m_msg = tb("m_msg", [P, D], F32)
            m_high = tb("m_high", [P, D + 2], F32R)
            m_low = tb("m_low", [P, D], F32R)

            b_rz = banks[0:2]
            b_pre, b_sum, b_mean, b_n, b_a = banks[2:7]
            b_xt, b_selt = banks[7][:, 0:D], banks[7][:, D:D + FAST * P]

            with nc.Block() as block:
                @block.sync
                def _(sp):
                    for q in range(FAST):
                        sp.dma_start(raw[:, q, :], table_rows[q * P:(q + 1) * P, :]).then_inc(rounds_there, 16)
                    rounds["SP"] = sp.value_load(rounds_i[0:1, 0:1], min_val=0, max_val=ROUNDS)
                    with sp.If(rounds["SP"] > FAST):
                        sp.wait_ge(free_made, 1)
                        with sp.Fori(FAST, rounds["SP"]) as q:
                            sp.dma_start(table_rows[bass.ds(q * P, P), :], free[:, :]).then_inc(rounds_there, 16)

                @block.tensor
                def _(pe):
                    nc.tensor.transpose(banks[1][:, 0:P], ident[:, :], ident[:, :]).then_inc(m_free, 1)
                    rounds["PE"] = pe.value_load(rounds_i[0:1, 0:1], min_val=0, max_val=ROUNDS)

                @block.scalar
                def _(act):
                    rounds["ACT"] = act.value_load(rounds_i[0:1, 0:1], min_val=0, max_val=ROUNDS)

                @block.gpsimd
                def _(pool):
                    nc.gpsimd.memset(msg_h[:, :, :, D:D + 2].bitcast(F32), 1.0)
                    nc.gpsimd.memset(m_high[:, D:D + 2].bitcast(F32), 1.0)
                    nc.gpsimd.memset(mean[:, :, 2 * P:3 * P], 0.0).then_inc(fixed_made, 1)
                    pool.wait_ge(fixed_made, 1)
                    nc.gpsimd.memset(mean[:, :, 2 * P + 2:2 * P + 4], 1.0)
                    nc.gpsimd.memset(xs[:, :, :], 0.0).then_inc(fixed_made, 1)
                    rounds["POOL"] = pool.value_load(rounds_i[0:1, 0:1], min_val=0, max_val=ROUNDS)

                    def scatter_again(v, first):
                        if not first:
                            pool.wait_ge(again_scattered, v * 32)
                        nc.gpsimd.tensor_tensor(spare[:, 1:2], lane[:, 0:1], lane[:, 0:1], ALU.add)
                        nc.gpsimd.tensor_copy(again[:, 0, :], index_all[:, bass.ds(2 * v, 2)])
                        nc.gpsimd.tensor_copy(again[:, 1, :], pay_all[:, bass.ds(2 * v, 2)]).then_inc(again_copied, 1)
                        pool.wait_ge(again_copied, v + 1)
                        nc.gpsimd.tensor_tensor(spare[:, 0:1], lane[:, 0:1], lane[:, 0:1], ALU.add)
                        for n in range(2):
                            pool.indirect_dma_start(table, bass.IndirectOffsetOnAxis(ap=again[:, 0, n:n + 1], axis=0),
                                                    again[:, 1, n:n + 1], None).then_inc(again_scattered, 16)

                    with pool.If(rounds["POOL"] > FAST):
                        pool.wait_ge(rounds_there, rounds["POOL"] * 16)
                        scatter_again(0, True)
                        with pool.Fori(1, PAIRS) as v:
                            scatter_again(v, False)
                        pool.wait_ge(again_scattered, 32 * PAIRS)

                @block.vector
                def _(dve):
                    dve.wait_ge(rounds_there, 16 * FAST)
                    nc.vector.tensor_scalar(slots[:, 0:FAST, :], raw[:, :, :], 0xFFFF, None, ALU.bitwise_and)
                    nc.vector.tensor_scalar(lanes_i[:, :, :], raw[:, :, :], 16, None, ALU.logical_shift_right).then_inc(decoded, 1)
                    dve.wait_ge(decoded, 1)
                    nc.vector.tensor_copy(slots[:, FAST:2 * FAST, :].bitcast(F32), lanes_i[:, :, :]).then_inc(decoded, 1)
                    rounds["DVE"] = dve.value_load(rounds_i[0:1, 0:1], min_val=0, max_val=ROUNDS)
                    with dve.If(rounds["DVE"] > FAST):
                        nc.vector.memset(free[:, :], EMPTY).then_inc(free_made, 1)
                        nc.vector.tensor_scalar(more_i[:, 0, :], banks[0][0:1, 0:NW], float(P - 1), None, ALU.add).then_inc(further_done, 1)
                        dve.wait_ge(further_done, 1)
                        nc.vector.tensor_scalar(more_i[:, 1, :], more_i[:, 0, :], 7, None, ALU.logical_shift_right).then_inc(further_done, 1)
                        dve.wait_ge(further_done, 2)
                        nc.vector.tensor_scalar(more_f[:, 0, :], more_i[:, 1, :], float(FAST), float(FAST), ALU.max, ALU.subtract).then_inc(further_done, 1)
                        nc.vector.memset(more_f[:, 2, :], 0.0).then_inc(further_done, 1)
                        dve.wait_ge(further_done, 4)
                        nc.vector.tensor_copy(further_i[:, 0, :], more_f[:, 0, :])
                        nc.vector.tensor_tensor_scan(more_f[:, 1, :], more_f[:, 0, :], more_f[:, 2, :], 0.0, ALU.add, ALU.add).then_inc(further_done, 1)
                        dve.wait_ge(further_done, 5)
                        nc.vector.tensor_tensor(further_i[:, 1, :], more_f[:, 1, :], more_f[:, 0, :], ALU.subtract).then_inc(further_done, 1)

            names = ("slot_ready sel_ready selt_copied xt_done xh_done xl_done a_done a_ready "
                     "pre_done pre_ready silu_done sum_done inv_done mean_ready mt_done mh_done ml_done hn_done rz_done n_done "
                     "trz_done u_done cand_in_done cand_done diff_done xbeta_done zd_done xn_done stats_done mv_done "
                     "arg1_done arg2_done minus_done rstd1_done rstd2_done shift_done g_done o_done stats2_done mv2_done out_ready silu_f_done msg_l_done ah_done "
                     "m_split m_dst_done m_lane_done m_sel_done m_selt_done m_selt_copied m_spread m_added m_silu_h_done "
                     "m_silu_done m_low_done").split()
            S = {n: sem(n) for n in names}
            x_loaded = [sem(f"x_loaded{n}") for n in range(XS)]
            gathered = [sem(f"gathered{n}") for n in range(3)]
            out_stored = [sem(f"out_stored{n}") for n in range(3)]
            m_loaded = sem("m_loaded")
            m_gathered = sem("m_gathered")

            def run(eng, stages, lo, hi):
                def step(u, c):
                    for off, stage in stages:
                        if c + off >= 0 and (c >= LO and not isinstance(u, int) or c + off < NT):
                            stage(u, c + off)
                for c in range(lo, LO):
                    step(0, c)
                with eng.Fori(0, LOOPS) as u:
                    for c in range(LO, LO + XS):
                        step(u, c)
                for c in range(HI, hi):
                    step(0, c)

            def in_turn(eng, stages, further, summed=None):
                def tile(u, c):
                    for stage in stages:
                        if stage is not further:
                            stage(u, c)
                            continue
                        number = eng.value_load(further_i[0:1, 0, bass.ds(XS * u + c, 1)], min_val=0, max_val=ROUNDS - FAST)
                        before = eng.value_load(further_i[0:1, 1, bass.ds(XS * u + c, 1)], min_val=0, max_val=ROUNDS - FAST)
                        with eng.If(number > 0):
                            with eng.Fori(0, number) as e:
                                further(u, c, before + e, e)
                        if summed:
                            summed(before + number)

                for c in range(XS):
                    tile(0, c)
                with eng.Fori(0, (NT - XS) // XS) as u:
                    for c in range(XS, 2 * XS):
                        tile(u, c)
                for c in range(NT // XS * XS, NT):
                    tile(0, c)

            def rows_of(c):
                return LAST_ROWS if c == NT - 1 else P

            def tile_rows(t, u, c):
                return t[bass.ds((XS * u + c) * P, rows_of(c)), :]

            LOAD, STORE = 4, -5
            with nc.Block() as block:
                @block.sync
                def _(sp):
                    def load(u, c):
                        if c >= XS:
                            sp.wait_ge(S["diff_done"], XS * u + (c - XS + 1))
                            sp.wait_ge(S["xbeta_done"], XS * u + (c - XS + 1))
                        sp.dma_start(xs[0:rows_of(c), c % XS, :], tile_rows(x, u, c)).then_inc(x_loaded[c % XS], 16)

                    def store(u, c):
                        sp.wait_ge(S["out_ready"], XS * u + (c + 1))
                        sp.dma_start(tile_rows(out, u, c), out_sb[0:rows_of(c), c % 3, :]).then_inc(out_stored[c % 3], 16)

                    def further(u, c, q, e):
                        sp.wait_ge(m_free, q + 1)
                        with nc.allow_non_contiguous_dma(reason="a column of the table"):
                            sp.dma_start(m_raw[:, :], table_rows[bass.ds((e + FAST) * P, P), bass.ds(XS * u + c, 1)]).then_inc(m_loaded, 16)

                    with sp.If(rounds["SP"] <= FAST):
                        run(sp, ((LOAD, load), (STORE, store)), -LOAD, NT - STORE)
                    with sp.Else():
                        in_turn(sp, (load, further, store), further)
                    for n in range(3):
                        sp.wait_ge(out_stored[n], 16 * len(range(n, NT, 3)))

                @block.tensor
                def _(pe):
                    def transposes(u, c):
                        pe.wait_ge(x_loaded[c % XS], 16 * u + 16 * (c // XS + 1))
                        pe.wait_ge(S["sel_ready"], XS * u + (c + 1))
                        if c >= 1:
                            pe.wait_ge(S["xl_done"], XS * u + c)
                            pe.wait_ge(S["selt_copied"], XS * u + c)
                        for k in range(KC):
                            nc.tensor.transpose(b_xt[:, k * P:(k + 1) * P], xs[:, c % XS, k * P:(k + 1) * P], ident[:, :])
                        for r in range(FAST):
                            last = nc.tensor.transpose(b_selt[:, r * P:(r + 1) * P], sel[:, c % 3, r, :].bitcast(F32), ident[:, :])
                        last.then_inc(S["xt_done"], 1)

                    def split_product(bank, high, low, weight, a, z, first, last):
                        n = 0
                        for left, right in ((high, weight[0]), (high, weight[1]), (low, weight[0])):
                            for k in range(KC):
                                mm = nc.tensor.matmul(bank, left(k), right[:, k, a:z], start=first and n == 0, stop=last and n == 5)
                                n += 1
                        return mm

                    def x_parts(c):
                        return (lambda k: xh[:, c % 2, k, :]), (lambda k: xl[:, c % 2, k, :])

                    def mean_parts(c):
                        return ((lambda k: mh[:, c % 2, k * P:(k + 1) * P]), (lambda k: ml[:, c % 2, k * P:(k + 1) * P]))

                    def source_product(u, c):
                        pe.wait_ge(S["xl_done"], XS * u + (c + 1))
                        if c >= 1:
                            pe.wait_ge(S["a_ready"], XS * u + c)
                        split_product(b_a[:, 0:D], *x_parts(c), w1a, 0, D, True, True).then_inc(S["a_done"], 1)

                    def hidden_gates(u, c):
                        if c >= 2:
                            pe.wait_ge(S["trz_done"], XS * u + (c - 1))
                        split_product(b_rz[c % 2][:, :], *x_parts(c), whh, 0, 2 * D, True, False)

                    def hidden_candidate(u, c):
                        if c >= 1:
                            pe.wait_ge(S["cand_in_done"], XS * u + c)
                        nc.tensor.matmul(b_n[:, D:2 * D], ones2[:, :], hn_bias[:, :], start=True, stop=False)
                        split_product(b_n[:, D:2 * D], *x_parts(c), whh, 2 * D, 3 * D, False, True).then_inc(S["hn_done"], 1)

                    def spread_sources(u, c):
                        pe.wait_ge(S["a_ready"], XS * u + (c + 1))
                        pe.wait_ge(S["selt_copied"], XS * u + (c + 1))
                        if c >= 1:
                            pe.wait_ge(S["pre_ready"], XS * u + c)
                        for r in range(FAST):
                            nc.tensor.matmul(b_pre[:, r * D:(r + 1) * D], sel_t[:, c % 3, r * P:(r + 1) * P], ah[:, c % 2, :], start=True, stop=False)
                            last = nc.tensor.matmul(b_pre[:, r * D:(r + 1) * D], sel_t[:, c % 3, r * P:(r + 1) * P], al[:, c % 2, :], start=False, stop=True)
                        last.then_inc(S["pre_done"], 1)

                    def sum_messages(u, c):
                        pe.wait_ge(S["msg_l_done"], XS * u + (c + 1))
                        if c >= 1:
                            pe.wait_ge(S["mean_ready"], XS * u + c)
                        for r in range(FAST):
                            nc.tensor.matmul(b_sum[:, 0:D + 2], sel[:, c % 3, r, :], msg_h[:, c % 2, r, :], start=(r == 0), stop=False)
                            last = nc.tensor.matmul(b_sum[:, 0:D], sel[:, c % 3, r, :], msg_l[:, c % 2, r, :], start=False, stop=(r == FAST - 1))
                        last.then_inc(S["sum_done"], 1)

                    def transpose_mean(u, c):
                        pe.wait_ge(S["mean_ready"], XS * u + (c + 1))
                        if c >= 1:
                            pe.wait_ge(S["ml_done"], XS * u + c)
                        for k in range(3):
                            last = nc.tensor.transpose(b_mean[:, k * P:(k + 1) * P], mean[:, c % 2, k * P:(k + 1) * P], ident[:, :])
                        last.then_inc(S["mt_done"], 1)

                    def input_gates(u, c):
                        pe.wait_ge(S["ml_done"], XS * u + (c + 1))
                        bias_rows = mh[0:4, c % 2, 2 * P:3 * P]
                        nc.tensor.matmul(b_rz[c % 2][:, :], bias_rows, gi_bias[:, 0:2 * D], start=False, stop=False)
                        split_product(b_rz[c % 2][:, :], *mean_parts(c), wc, 0, 2 * D, False, True).then_inc(S["rz_done"], 1)
                        nc.tensor.matmul(b_n[:, 0:D], bias_rows, gi_bias[:, 2 * D:3 * D], start=True, stop=False)
                        split_product(b_n[:, 0:D], *mean_parts(c), wc, 2 * D, 3 * D, False, True).then_inc(S["n_done"], 1)

                    def further(u, c, q, e):
                        pe.wait_ge(S["m_sel_done"], q + 1)
                        nc.tensor.transpose(b_selt[:, 0:P], m_sel[:, :].bitcast(F32), ident[:, :]).then_inc(S["m_selt_done"], 1)
                        pe.wait_ge(S["m_selt_copied"], q + 1)
                        nc.tensor.matmul(b_pre[:, 0:D], m_sel_t[:, :], ah[:, c % 2, :], start=True, stop=False)
                        nc.tensor.matmul(b_pre[:, 0:D], m_sel_t[:, :], al[:, c % 2, :], start=False, stop=True).then_inc(S["m_spread"], 1)
                        pe.wait_ge(S["m_low_done"], q + 1)
                        nc.tensor.matmul(b_sum[:, 0:D + 2], m_sel[:, :], m_high[:, :], start=False, stop=False, skip_group_check=True)
                        nc.tensor.matmul(b_sum[:, 0:D], m_sel[:, :], m_low[:, :], start=False, stop=True, skip_group_check=True).then_inc(m_free, 1)

                    with pe.If(rounds["PE"] <= FAST):
                        run(pe, ((0, spread_sources), (-1, transpose_mean), (0, hidden_gates), (-1, input_gates), (1, source_product), (0, sum_messages),
                                 (2, transposes), (0, hidden_candidate)), -2, NT + 1)
                    with pe.Else():
                        in_turn(pe, (transposes, source_product, spread_sources, hidden_gates, sum_messages, further,
                                     transpose_mean, hidden_candidate, input_gates), further)

                @block.scalar
                def _(act):
                    def mean_high(u, c):
                        act.wait_ge(S["mt_done"], XS * u + (c + 1))
                        if c >= 2:
                            act.wait_ge(S["n_done"], XS * u + (c - 1))
                        nc.scalar.activation(mh[:, c % 2, :], b_mean[:, 0:3 * P], ACT.Copy).then_inc(S["mh_done"], 1)

                    def x_high(u, c):
                        act.wait_ge(S["xt_done"], XS * u + (c + 1))
                        if c >= 2:
                            act.wait_ge(S["hn_done"], XS * u + (c - 1))
                        nc.scalar.activation(xh[:, c % 2, :, :].rearrange("p k n -> p (k n)"), b_xt, ACT.Copy).then_inc(S["xh_done"], 1)

                    def silu(u, c):
                        act.wait_ge(S["pre_ready"], XS * u + (c + 1))
                        if c >= 2:
                            act.wait_ge(S["sum_done"], XS * u + (c - 1))
                        rows_of_pre = pre[:, c % 2, :].rearrange("p (r d) -> p r d", r=FAST)
                        nc.scalar.activation(msg_h[:, c % 2, :, 0:D], rows_of_pre, ACT.Silu).then_inc(S["silu_done"], 1)
                        if c >= 1:
                            act.wait_ge(S["msg_l_done"], XS * u + c)
                        nc.scalar.activation(msg[:, :, :], rows_of_pre, ACT.Silu).then_inc(S["silu_f_done"], 1)

                    def gates(u, c):
                        act.wait_ge(S["rz_done"], XS * u + (c + 1))
                        if c >= 2:
                            act.wait_ge(S["xn_done"], XS * u + (c - 1))
                        nc.scalar.activation(trz[:, c % 2, :], b_rz[c % 2][:, :], ACT.Tanh, scale=0.5).then_inc(S["trz_done"], 1)

                    def copy_sel_t(u, c):
                        act.wait_ge(S["xt_done"], XS * u + (c + 1))
                        if c >= 3:
                            act.wait_ge(S["pre_done"], XS * u + (c - 2))
                        nc.scalar.activation(sel_t[:, c % 3, :], b_selt, ACT.Copy).then_inc(S["selt_copied"], 1)

                    def candidate(u, c):
                        act.wait_ge(S["cand_in_done"], XS * u + (c + 1))
                        if c >= 2:
                            act.wait_ge(S["xn_done"], XS * u + (c - 1))
                        nc.scalar.activation(cand[:, c % 2, :], cand_in[:, c % 2, :], ACT.Tanh).then_inc(S["cand_done"], 1)

                    def source_high(u, c):
                        act.wait_ge(S["a_done"], XS * u + (c + 1))
                        if c >= 2:
                            act.wait_ge(S["pre_done"], XS * u + (c - 1))
                        nc.scalar.activation(ah[:, c % 2, :], b_a[:, 0:D], ACT.Copy).then_inc(S["ah_done"], 1)

                    def scale_sum(u, c):
                        act.wait_ge(S["inv_done"], 2 * XS * u + (2 * c + 2))
                        nc.scalar.activation(mean[:, c % 2, 0:D], b_sum[:, 0:D], ACT.Copy, scale=inv[:, 1, c % 2:c % 2 + 1]).then_inc(S["mean_ready"], 1)

                    def second_norm(u, c):
                        act.wait_ge(S["shift_done"], XS * u + (c + 1))
                        if c >= 3:
                            act.wait_ge(out_stored[c % 3], 32 * u + 16 * (c // 3))
                        nc.scalar.activation(out_sb[:, c % 3, :], o_sb[:, c % 3, :], ACT.Identity, bias=shift[:, c % 3:c % 3 + 1],
                                             scale=rstd[:, 1, c % 3:c % 3 + 1]).then_inc(S["out_ready"], 1)

                    def further(u, c, q, e):
                        act.wait_ge(S["m_selt_done"], q + 1)
                        nc.scalar.activation(m_sel_t[:, :], b_selt[:, 0:P], ACT.Copy).then_inc(S["m_selt_copied"], 1)
                        act.wait_ge(S["m_added"], q + 1)
                        nc.scalar.activation(m_high[:, 0:D], m_pre[:, :], ACT.Silu).then_inc(S["m_silu_h_done"], 1)
                        nc.scalar.activation(m_msg[:, :], m_pre[:, :], ACT.Silu).then_inc(S["m_silu_done"], 1)

                    with act.If(rounds["ACT"] <= FAST):
                        run(act, ((-1, mean_high), (1, x_high), (1, copy_sel_t), (0, silu), (-5, second_norm), (-1, gates),
                                  (1, source_high), (-1, candidate), (0, scale_sum)), -1, NT + 5)
                    with act.Else():
                        in_turn(act, (x_high, copy_sel_t, source_high, silu, further, scale_sum, mean_high, gates, candidate,
                                      second_norm), further)

                @block.vector
                def _(dve):
                    def mean_low(u, c):
                        dve.wait_ge(S["mh_done"], XS * u + (c + 1))
                        nc.vector.tensor_tensor(ml[:, c % 2, :], b_mean[:, 0:2 * P], mh[:, c % 2, 0:2 * P], ALU.subtract).then_inc(S["ml_done"], 1)

                    def x_low(u, c):
                        dve.wait_ge(S["xh_done"], XS * u + (c + 1))
                        dve.wait_ge(S["selt_copied"], XS * u + (c + 1))
                        nc.vector.tensor_tensor(xl[:, c % 2, :, :].rearrange("p k n -> p (k n)"), b_xt,
                                                xh[:, c % 2, :, :].rearrange("p k n -> p (k n)"), ALU.subtract).then_inc(S["xl_done"], 1)

                    def add_destinations(u, c):
                        dve.wait_ge(S["pre_done"], XS * u + (c + 1))
                        dve.wait_ge(gathered[c % 3], 64 * u + 32 * (c // 3 + 1))
                        if c >= 2:
                            dve.wait_ge(S["silu_f_done"], XS * u + (c - 1))
                        nc.vector.tensor_tensor(pre[:, c % 2, :], b_pre[:, :], got[:, c % 3, :], ALU.add).then_inc(S["pre_ready"], 1)

                    def select(u, c):
                        dve.wait_ge(S["slot_ready"], XS * u + (c + 1))
                        if c >= 3:
                            dve.wait_ge(S["sum_done"], XS * u + (c - 2))
                        for r in range(FAST):
                            last = nc.vector.tensor_scalar(sel[:, c % 3, r, :], lane[:, :], slot[:, c % 3, FAST + r:FAST + r + 1].bitcast(F32), None, ALU.is_equal)
                        last.then_inc(S["sel_ready"], 1)

                    def reset_gate(u, c):
                        dve.wait_ge(S["trz_done"], XS * u + (c + 1))
                        dve.wait_ge(S["n_done"], XS * u + (c + 1))
                        nc.vector.scalar_tensor_tensor(out=u_sb[:, c % 2, :], in0=trz[:, c % 2, 0:D], scalar=1.0, in1=b_n[:, D:2 * D],
                                                       op0=ALU.add, op1=ALU.mult).then_inc(S["u_done"], 1)

                    def candidate_input(u, c):
                        dve.wait_ge(S["u_done"], XS * u + (c + 1))
                        if c >= 2:
                            dve.wait_ge(S["cand_done"], XS * u + (c - 1))
                        nc.vector.scalar_tensor_tensor(out=cand_in[:, c % 2, :], in0=u_sb[:, c % 2, :], scalar=0.5, in1=b_n[:, 0:D],
                                                       op0=ALU.mult, op1=ALU.add).then_inc(S["cand_in_done"], 1)

                    def source_low(u, c):
                        dve.wait_ge(S["ah_done"], XS * u + (c + 1))
                        nc.vector.tensor_tensor(al[:, c % 2, :], b_a[:, 0:D], ah[:, c % 2, :].bitcast(F32), ALU.subtract).then_inc(S["a_ready"], 1)

                    def gated_difference(u, c):
                        dve.wait_ge(S["diff_done"], XS * u + (c + 1))
                        nc.vector.scalar_tensor_tensor(out=zd[:, c % 2, :], in0=trz[:, c % 2, D:2 * D], scalar=1.0, in1=diff[:, c % 2, :],
                                                       op0=ALU.add, op1=ALU.mult).then_inc(S["zd_done"], 1)

                    def new_state(u, c):
                        dve.wait_ge(S["zd_done"], XS * u + (c + 1))
                        nc.vector.scalar_tensor_tensor(out=xn[:, c % 3, :], in0=zd[:, c % 2, :], scalar=0.5, in1=cand[:, c % 2, :],
                                                       op0=ALU.mult, op1=ALU.add).then_inc(S["xn_done"], 1)

                    def state_stats(u, c):
                        dve.wait_ge(S["xn_done"], XS * u + (c + 1))
                        nc.vector.bn_stats(stats[:, 0, :], xn[:, c % 3, :]).then_inc(S["stats_done"], 1)

                    def state_stats_there(u, c):
                        dve.wait_ge(S["stats_done"], XS * u + (c + 1))

                    def state_moments(u, c):
                        nc.vector.bn_aggr(mv[:, 0, c % 3, :], stats[:, 0, :]).then_inc(S["mv_done"], 1)

                    def number(u, c):
                        dve.wait_ge(S["sum_done"], XS * u + (c + 1))
                        if c >= 2:
                            dve.wait_ge(S["mt_done"], XS * u + (c - 1))
                        nc.vector.tensor_scalar(mean[:, c % 2, 2 * P:2 * P + 2], b_sum[:, D:D + 2], 1.0, None, ALU.min)
                        nc.vector.tensor_scalar(inv[:, 0, c % 2:c % 2 + 1], b_sum[:, D:D + 1], 1e-8, None, ALU.add).then_inc(S["inv_done"], 1)

                    def inverse(u, c):
                        dve.wait_ge(S["inv_done"], 2 * XS * u + (2 * c + 1))
                        nc.vector.reciprocal(inv[:, 1, c % 2:c % 2 + 1], inv[:, 0, c % 2:c % 2 + 1]).then_inc(S["inv_done"], 1)

                    def norm_gamma(u, c):
                        dve.wait_ge(S["rstd1_done"], XS * u + (c + 1))
                        nc.vector.scalar_tensor_tensor(out=g_sb[:, c % 2, :], in0=xn[:, c % 3, :], scalar=mv[:, 0, c % 3, 0:1], in1=gamma_b[:, :],
                                                       op0=ALU.subtract, op1=ALU.mult).then_inc(S["g_done"], 1)

                    def add_beta(u, c):
                        dve.wait_ge(x_loaded[c % XS], 16 * u + 16 * (c // XS + 1))
                        if c >= 3:
                            dve.wait_ge(S["o_done"], XS * u + (c - 2))
                        nc.vector.tensor_tensor(xbeta[:, c % 3, :], xs[:, c % XS, :], beta_b[:, :], ALU.add).then_inc(S["xbeta_done"], 1)

                    def residual(u, c):
                        dve.wait_ge(S["g_done"], XS * u + (c + 1))
                        dve.wait_ge(S["xbeta_done"], XS * u + (c + 1))
                        if c >= 3:
                            dve.wait_ge(S["out_ready"], XS * u + (c - 2))
                        nc.vector.scalar_tensor_tensor(out=o_sb[:, c % 3, :], in0=g_sb[:, c % 2, :], scalar=rstd[:, 0, c % 3:c % 3 + 1], in1=xbeta[:, c % 3, :],
                                                       op0=ALU.mult, op1=ALU.add).then_inc(S["o_done"], 1)

                    def residual_stats(u, c):
                        dve.wait_ge(S["o_done"], XS * u + (c + 1))
                        nc.vector.bn_stats(stats[:, 1, :], o_sb[:, c % 3, :]).then_inc(S["stats2_done"], 1)

                    def residual_stats_there(u, c):
                        dve.wait_ge(S["stats2_done"], XS * u + (c + 1))

                    def residual_moments(u, c):
                        nc.vector.bn_aggr(mv[:, 1, c % 3, :], stats[:, 1, :]).then_inc(S["mv2_done"], 1)

                    def apart(u, c):
                        nc.vector.memset(spare_v[:, :], 0.0)

                    def further(u, c, q, e):
                        dve.wait_ge(m_free, q + 1)
                        dve.wait_ge(m_loaded, q * 16 + 16)
                        nc.vector.tensor_scalar(m_dst[:, :], m_raw[:, :], 0xFFFF, None, ALU.bitwise_and).then_inc(S["m_dst_done"], 1)
                        nc.vector.tensor_scalar(m_lane_i[:, :], m_raw[:, :], 16, None, ALU.logical_shift_right).then_inc(S["m_split"], 1)
                        dve.wait_ge(S["m_split"], q + 1)
                        nc.vector.tensor_copy(m_lane[:, :], m_lane_i[:, :]).then_inc(S["m_lane_done"], 1)
                        dve.wait_ge(S["m_lane_done"], q + 1)
                        nc.vector.tensor_scalar(m_sel[:, :], lane[:, :], m_lane[:, :], None, ALU.is_equal).then_inc(S["m_sel_done"], 1)
                        dve.wait_ge(S["m_spread"], q + 1)
                        dve.wait_ge(m_gathered, q * 16 + 16)
                        nc.vector.tensor_tensor(m_pre[:, :], b_pre[:, 0:D], m_got[:, :], ALU.add).then_inc(S["m_added"], 1)

                    def summed(q):
                        dve.wait_ge(m_free, q + 1)

                    with dve.If(rounds["DVE"] <= FAST):
                        run(dve, ((-4, residual_stats_there), (0, add_destinations), (-4, residual_moments), (-1, mean_low),
                                  (-2, gated_difference), (2, select), (-2, new_state), (1, x_low), (-2, state_stats), (-1, add_beta),
                                  (-2, state_stats_there), (-1, reset_gate), (-2, state_moments), (-1, candidate_input),
                                  (-3, norm_gamma), (0, number), (1, source_low), (0, inverse), (-3, residual),
                                  (-3, residual_stats)), -2, NT + 4)
                    with dve.Else():
                        in_turn(dve, (select, x_low, source_low, add_destinations, further, number, inverse, mean_low, reset_gate,
                                      candidate_input, gated_difference, new_state, state_stats, state_stats_there, apart, state_moments,
                                      norm_gamma, add_beta, residual, residual_stats, residual_stats_there, apart, residual_moments),
                                further, summed)

                @block.gpsimd
                def _(pool):
                    def fetch_slot(u, c):
                        if c >= 3:
                            pool.wait_ge(S["sel_ready"], XS * u + (c - 2))
                            pool.wait_ge(S["pre_ready"], XS * u + (c - 2))
                        nc.gpsimd.tensor_copy(slot[:, c % 3, :], slots[:, :, bass.ds(XS * u + c, 1)].rearrange("p r a -> p (r a)")).then_inc(S["slot_ready"], 1)

                    def slot_there(u, c):
                        pool.wait_ge(S["slot_ready"], XS * u + (c + 1))

                    def gather(u, c):
                        for r in range(FAST):
                            pool.indirect_dma_start(got[:, c % 3, r * D:(r + 1) * D], None, xb_rows,
                                                    bass.IndirectOffsetOnAxis(ap=slot[:, c % 3, r:r + 1], axis=0)).then_inc(gathered[c % 3], 16)

                    def differ(u, c):
                        pool.wait_ge(S["cand_done"], XS * u + (c + 1))
                        if c >= 2:
                            pool.wait_ge(S["zd_done"], XS * u + (c - 1))
                        nc.gpsimd.tensor_tensor(diff[:, c % 2, :], xs[:, c % XS, :], cand[:, c % 2, :], ALU.subtract).then_inc(S["diff_done"], 1)

                    def message_low(u, c):
                        pool.wait_ge(S["silu_f_done"], XS * u + (c + 1))
                        if c >= 2:
                            pool.wait_ge(S["sum_done"], XS * u + (c - 1))
                        nc.gpsimd.tensor_tensor(msg_l[:, c % 2, :, :], msg[:, :, :], msg_h[:, c % 2, :, 0:D].bitcast(F32), ALU.subtract).then_inc(S["msg_l_done"], 1)

                    def argument(u, c, norm, there, done):
                        pool.wait_ge(there, XS * u + (c + 1))
                        nc.gpsimd.tensor_tensor(arg[:, norm, c % 3:c % 3 + 1], mv[:, norm, c % 3, 1:2], columns[:, 1:2], ALU.add).then_inc(done, 1)

                    def root(u, c, norm, there, done):
                        pool.wait_ge(there, XS * u + (c + 1))
                        nc.gpsimd.tensor_tensor(rstd[:, norm, c % 3:c % 3 + 1], arg[:, norm, c % 3:c % 3 + 1], columns[:, 0:1], ALU.pow).then_inc(done, 1)

                    def state_argument(u, c):
                        argument(u, c, 0, S["mv_done"], S["arg1_done"])

                    def state_root(u, c):
                        root(u, c, 0, S["arg1_done"], S["rstd1_done"])

                    def residual_argument(u, c):
                        argument(u, c, 1, S["mv2_done"], S["arg2_done"])
                        nc.gpsimd.tensor_tensor(minus_mean[:, c % 3:c % 3 + 1], mv[:, 1, c % 3, 0:1], columns[:, 2:3], ALU.mult).then_inc(S["minus_done"], 1)

                    def residual_root(u, c):
                        root(u, c, 1, S["arg2_done"], S["rstd2_done"])

                    def shift_row(u, c):
                        pool.wait_ge(S["minus_done"], XS * u + (c + 1))
                        pool.wait_ge(S["rstd2_done"], XS * u + (c + 1))
                        nc.gpsimd.tensor_tensor(shift[:, c % 3:c % 3 + 1], minus_mean[:, c % 3:c % 3 + 1], rstd[:, 1, c % 3:c % 3 + 1], ALU.mult).then_inc(S["shift_done"], 1)

                    def apart(u, c):
                        nc.gpsimd.tensor_tensor(spare[:, 1:2], lane[:, 0:1], lane[:, 0:1], ALU.add)

                    def further(u, c, q, e):
                        pool.wait_ge(S["m_dst_done"], q + 1)
                        nc.gpsimd.tensor_tensor(spare[:, 0:1], lane[:, 0:1], lane[:, 0:1], ALU.add)
                        pool.indirect_dma_start(m_got[:, :], None, xb_rows,
                                                bass.IndirectOffsetOnAxis(ap=m_dst[:, :], axis=0)).then_inc(m_gathered, 16)
                        pool.wait_ge(S["m_silu_h_done"], q + 1)
                        pool.wait_ge(S["m_silu_done"], q + 1)
                        nc.gpsimd.tensor_tensor(m_low[:, :], m_msg[:, :], m_high[:, 0:D].bitcast(F32), ALU.subtract).then_inc(S["m_low_done"], 1)

                    with pool.If(rounds["POOL"] <= FAST):
                        run(pool, ((2, slot_there), (-5, shift_row), (2, gather), (0, message_low), (-4, residual_argument),
                                   (-4, residual_root), (-2, state_argument), (-2, state_root), (-1, differ), (3, fetch_slot)),
                            -3, NT + 5)
                    with pool.Else():
                        in_turn(pool, (fetch_slot, slot_there, apart, gather, message_low, further, differ,
                                       state_argument, state_root, residual_argument, residual_root, shift_row), further)


_INS = ['x', 'src', 'dst', 'L0_gnn_W1', 'L0_gnn_b1', 'L0_gnn_W2', 'L0_gnn_b2', 'L0_gnn_w_ih', 'L0_gnn_w_hh',
        'L0_gnn_b_ih', 'L0_gnn_b_hh', 'L0_gnn_gamma', 'L0_gnn_beta']


def kernel(**inputs):
    import numpy as _np
    import concourse.bacc as _bacc
    from concourse import mybir as _mybir
    from concourse.bass_utils import run_bass_kernel_spmd as _run

    nc = _bacc.Bacc("TRN2", target_bir_lowering=False, num_devices=1)
    arrays, args = {}, []
    for name in _INS:
        a = _np.ascontiguousarray(inputs[name])
        arrays[f"in_{name}_dram"] = a
        args.append(nc.dram_tensor(f"in_{name}_dram", a.shape, _mybir.dt.from_np(a.dtype), kind="ExternalInput").ap())
    out = nc.dram_tensor("out_0_dram", (N, D), F32, kind="ExternalOutput").ap()
    build(nc, *args, out)
    r = _run(nc, [arrays], core_ids=[0])
    return r.results[0]["out_0_dram"]
```

```python
from contextlib import ExitStack

import concourse.bass as bass
from concourse import mybir

F32 = mybir.dt.float32
F32R = mybir.dt.float32r
F16 = mybir.dt.float16
I32 = mybir.dt.int32
ALU = mybir.AluOpType
ACT = mybir.ActivationFunctionType
AX = mybir.AxisListType

P = 128
N, D = 50000, 256
E = 75000
NT = -(-N // P)
LAST_ROWS = N - (NT - 1) * P
KC = D // P
EC = -(-E // P)
ES = 9
TW = 1 << ES
ROUND = P * TW
FAST = 2
ROUNDS = -(-E // P)
EMPTY = 255 << 16
NW = NT + 1
PAIRS = EC // 2
MT, MP = 4, 3
MACROS = -(-NT // MT)
MACROS_UNROLL = 4
MACROS_FIRST = 2 + (MACROS - 3) % MACROS_UNROLL
LAST_MT = NT - (MACROS - 1) * MT
LAST_MP = PAIRS - (MACROS - 1) * MP
TAIL = N - (MACROS - 1) * MT * P
TAIL_P = TAIL // LAST_MT
assert TAIL_P * LAST_MT == TAIL and EC == 2 * PAIRS and 0 < LAST_MP <= MP
XS = 6
LO = 8
LOOPS = (NT - 1 - 4 - LO) // XS
HI = LO + XS * LOOPS
EPS = 1e-5


def build(nc, x, src, dst, W1, b1, W2, b2, w_ih, w_hh, b_ih, b_hh, gamma, beta, out):
    ctx = ExitStack()
    with ctx:
        def sb(name, shape, dt):
            return ctx.enter_context(nc.sbuf_tensor("sb_" + name, shape, dt))

        def sem(name):
            return ctx.enter_context(nc.semaphore(name))

        xb_rows = nc.dram_tensor("xb_rows", [N, D], F32, kind="Internal").ap()
        table = nc.dram_tensor("edge_table", [ROUNDS * ROUND, 1], I32, kind="Internal").ap()

        banks = [ctx.enter_context(nc.psum_tensor(f"bank{n}", [P, 512], F32)) for n in range(8)]

        ident = sb("ident", [P, P], F32)
        ident16 = sb("ident16", [P, P], F16)
        lane = sb("lane", [P, P], F32)
        lane16 = sb("lane16", [P, P], F16)
        gamma_b = sb("gamma_b", [P, D], F32)
        beta_b = sb("beta_b", [P, D], F32)
        w1a = [sb(f"w1a{n}", [P, KC, D], F32R) for n in range(2)]
        w1b = [sb(f"w1b{n}", [P, KC, D], F32R) for n in range(2)]
        whh = [sb(f"whh{n}", [P, KC, 3 * D], F32R) for n in range(2)]
        wc = [sb(f"wc{n}", [P, KC, 3 * D], F32R) for n in range(2)]
        gi_bias = sb("gi_bias", [4, 3 * D], F32R)
        hn_bias = sb("hn_bias", [2, D], F32R)
        ones2 = sb("ones2", [2, P], F32R)
        columns = sb("columns", [P, 3], F32)
        slots = sb("slots", [P, 2 * FAST, TW], I32)
        index_all = sb("index_all", [P, EC + 2], I32)
        pay_all = sb("pay_all", [P, EC + 2], I32)
        rounds_i = sb("rounds_i", [P, 1], I32)
        w2_raw = sb("w2_raw", [P, 2, D], F32)
        wih_t = sb("wih_t", [P, KC, 3 * D], F32)
        b2_col = sb("b2_col", [P, KC], F32)
        b2w_high = sb("b2w_high", [1, 3 * D], F32R)
        b2w_low = sb("b2w_low", [1, 3 * D], F32R)
        flat = lambda t: t[:, :, :].rearrange("p k n -> p (k n)")

        stage2 = ctx.enter_context(ExitStack())

        def t2(name, shape, dt):
            return stage2.enter_context(nc.sbuf_tensor("sb_" + name, shape, dt))

        src_i = t2("src_i", [P, EC], I32)
        dst_i = t2("dst_i", [P, EC], I32)
        tile_i = t2("tile_i", [P, EC + 2], I32)
        tile_f = t2("tile_f", [P, EC + 2], F32)
        tiles16 = t2("tiles16", [P, NW], F16)
        tri = t2("tri", [P, P], F16)
        rest = t2("rest", [P, P], F16)
        ones16 = t2("ones16", [P, P], F16)
        c_high = t2("c_high", [1, 4 * D], F32R)
        c_low = t2("c_low", [1, 4 * D], F32R)
        b1_wide = t2("b1_wide", [P, D], F32)
        empty = t2("empty", [P, FAST * ROUND // P], I32)
        x2 = t2("x2", [P, 2, MT, D], F32)
        FULL = E // EC
        REST = E - FULL * EC

        const_made = sem("const_made")
        w1_loaded = sem("w1_loaded")
        whh_loaded = sem("whh_loaded")
        wih_loaded = sem("wih_loaded")
        biases_loaded = sem("biases_loaded")
        late_loaded = sem("late_loaded")
        w_transposed = sem("w_transposed")
        w_high = sem("w_high")
        rows_ready = sem("rows_ready")
        rows_high = sem("rows_high")
        rows_low = sem("rows_low")
        b1_loaded = sem("b1_loaded")
        rows_placed = sem("rows_placed")
        edges_loaded = sem("edges_loaded")
        pads_made = sem("pads_made")
        tri_made = sem("tri_made")
        prep = sem("prep")
        empty_made = sem("empty_made")
        table_cleared = sem("table_cleared")
        x_in = [sem(f"x_in{n}") for n in range(2)]
        with ExitStack() as tmp:
            def tb(name, shape, dt):
                return tmp.enter_context(nc.sbuf_tensor("sb_" + name, shape, dt))

            w1_raw = tb("w1_raw", [P, 2, 2 * D], F32)
            whh_raw = tb("whh_raw", [P, 6, D], F32)
            wih_raw = tb("wih_raw", [P, 6, D], F32)
            bi_row = tb("bi_row", [1, 3 * D], F32)
            bh_row = tb("bh_row", [1, 3 * D], F32)
            c_row = tb("c_row", [1, 4 * D], F32)
            ones_f = tb("ones_f", [2, P], F32)

            banks_of = []
            for raw, loaded, chunk, target, width in ((w1_raw, w1_loaded, D, w1b, D), (w1_raw, w1_loaded, 0, w1a, D),
                                                      (whh_raw, whh_loaded, 0, whh, 3 * D), (wih_raw, wih_loaded, 0, None, 3 * D)):
                blocks = [(raw, o, chunk + k * P) for k in range(KC) for o in range(width // P)]
                for n in range(0, len(blocks), 4):
                    banks_of.append((loaded, target, n * P, blocks[n:n + 4]))
            assert len(banks_of) == 8

            with nc.Block() as block:
                @block.sync
                def _(sp):
                    sp.dma_start(w1_raw[:, :, :], W1.rearrange("(o p) k -> p o k", p=P)).then_inc(w1_loaded, 16)
                    sp.dma_start(bi_row[:, :], b_ih.rearrange("(a n) -> a n", a=1)).then_inc(biases_loaded, 16)
                    sp.dma_start(bh_row[:, :], b_hh.rearrange("(a n) -> a n", a=1)).then_inc(biases_loaded, 16)
                    sp.wait_ge(pads_made, 1)
                    sp.dma_start(src_i[0:FULL, :], src[0:FULL * EC].rearrange("(p c) -> p c", c=EC)).then_inc(edges_loaded, 16)
                    sp.dma_start(dst_i[0:FULL, :], dst[0:FULL * EC].rearrange("(p c) -> p c", c=EC)).then_inc(edges_loaded, 16)
                    sp.dma_start(src_i[FULL:P, 0:REST], src[FULL * EC:E].rearrange("(p c) -> p c", p=1)).then_inc(edges_loaded, 16)
                    sp.dma_start(dst_i[FULL:P, 0:REST], dst[FULL * EC:E].rearrange("(p c) -> p c", p=1)).then_inc(edges_loaded, 16)
                    sp.dma_start(whh_raw[:, :, :], w_hh.rearrange("(o p) k -> p o k", p=P)).then_inc(whh_loaded, 16)
                    sp.dma_start(wih_raw[:, :, :], w_ih.rearrange("(o p) k -> p o k", p=P)).then_inc(wih_loaded, 16)
                    for c in range(2):
                        sp.dma_start(x2[:, c, :, :], x[c * MT * P:(c + 1) * MT * P, :].rearrange("(p q) d -> p q d", q=MT)).then_inc(x_in[c], 16)
                    sp.wait_ge(empty_made, 1)
                    sp.dma_start(table[0:FAST * ROUND, :].rearrange("(p n) a -> p (n a)", p=P), empty[:, :]).then_inc(table_cleared, 16)
                    sp.dma_start(w2_raw[:, :, :], W2.rearrange("(o p) k -> p o k", p=P)).then_inc(late_loaded, 16)
                    with nc.allow_non_contiguous_dma(reason="256 values, once"):
                        sp.dma_start(b2_col[:, :], b2.rearrange("(c p) -> p c", p=P)).then_inc(late_loaded, 16)
                    sp.dma_start(b1_wide[:, :], b1.rearrange("(a n) -> a n", a=1).to_broadcast([P, D])).then_inc(b1_loaded, 16)
                    for row, wide in ((gamma, gamma_b), (beta, beta_b)):
                        sp.dma_start(wide[:, :], row.rearrange("(a n) -> a n", a=1).to_broadcast([P, D])).then_inc(late_loaded, 16)
                    sp.wait_ge(rows_low, 1)
                    sp.dma_start(gi_bias[2:3, :].bitcast(F32), c_high[:, 0:3 * D].bitcast(F32)).then_inc(rows_placed, 16)
                    sp.dma_start(gi_bias[3:4, :].bitcast(F32), c_low[:, 0:3 * D].bitcast(F32)).then_inc(rows_placed, 16)
                    sp.dma_start(hn_bias[0:1, :].bitcast(F32), c_high[:, 3 * D:4 * D].bitcast(F32)).then_inc(rows_placed, 16)
                    sp.dma_start(hn_bias[1:2, :].bitcast(F32), c_low[:, 3 * D:4 * D].bitcast(F32)).then_inc(rows_placed, 16)

                @block.gpsimd
                def _(pool):
                    nc.gpsimd.iota(src_i[:, :], [[P, EC]], base=(NW + 8 - REST) * P, channel_multiplier=0)
                    nc.gpsimd.memset(dst_i[:, :], 0).then_inc(pads_made, 1)
                    nc.gpsimd.memset(ident[:, :], 0.0).then_inc(const_made, 1)
                    pool.wait_ge(const_made, 1)
                    nc.gpsimd.affine_select(out=ident[:, :], in_=ident[:, :], compare_op=ALU.not_equal, fill=1.0,
                                            base=0, pattern=[[-1, P]], channel_multiplier=1).then_inc(const_made, 1)
                    nc.gpsimd.iota(lane[:, :], [[1, P]], base=0, channel_multiplier=0,
                                   allow_small_or_imprecise_dtypes=True).then_inc(const_made, 1)
                    nc.gpsimd.iota(lane16[:, :], [[1, P]], base=0, channel_multiplier=0,
                                   allow_small_or_imprecise_dtypes=True)
                    pool.wait_ge(const_made, 2)
                    nc.gpsimd.tensor_copy(ident16[:, :], ident[:, :])
                    nc.gpsimd.memset(columns[:, 0:1], -0.5)
                    nc.gpsimd.memset(columns[:, 1:2], EPS)
                    nc.gpsimd.memset(columns[:, 2:3], -1.0)
                    nc.gpsimd.iota(tiles16[:, :], [[1, NW]], base=0, channel_multiplier=0,
                                   allow_small_or_imprecise_dtypes=True)
                    nc.gpsimd.memset(tri[:, :], 1.0)
                    nc.gpsimd.memset(rest[:, :], 1.0)
                    nc.gpsimd.memset(ones16[:, :], 1.0).then_inc(tri_made, 1)
                    pool.wait_ge(tri_made, 1)
                    nc.gpsimd.affine_select(out=tri[:, :], in_=tri[:, :], compare_op=ALU.is_gt, fill=0.0,
                                            base=0, pattern=[[1, P]], channel_multiplier=-1)
                    nc.gpsimd.affine_select(out=rest[:, :], in_=rest[:, :], compare_op=ALU.is_ge, fill=0.0,
                                            base=0, pattern=[[-1, P]], channel_multiplier=1).then_inc(tri_made, 1)

                @block.tensor
                def _(pe):
                    pe.wait_ge(const_made, 2)
                    for n, (loaded, _, _, blocks) in enumerate(banks_of):
                        pe.wait_ge(loaded, 16)
                        for b, (raw, o, col) in enumerate(blocks):
                            last = nc.tensor.transpose(banks[n][:, b * P:(b + 1) * P], raw[:, o, col:col + P], ident[:, :])
                        last.then_inc(w_transposed, 1)

                @block.scalar
                def _(act):
                    act.wait_ge(rows_ready, 3)
                    nc.scalar.activation(c_high[:, :], c_row[:, :], ACT.Copy).then_inc(rows_high, 1)
                    for n, (_, target, col, _) in enumerate(banks_of):
                        act.wait_ge(w_transposed, n + 1)
                        if target is None:
                            nc.scalar.activation(flat(wih_t)[:, col:col + 512], banks[n][:, :], ACT.Copy)
                        else:
                            nc.scalar.activation(flat(target[0])[:, col:col + 512], banks[n][:, :], ACT.Copy).then_inc(w_high, 1)

                @block.vector
                def _(dve):
                    nc.vector.memset(empty[:, :], EMPTY).then_inc(empty_made, 1)
                    nc.vector.memset(ones_f[:, :], 1.0).then_inc(rows_ready, 1)
                    dve.wait_ge(biases_loaded, 32)
                    nc.vector.tensor_tensor(c_row[:, 0:2 * D], bi_row[:, 0:2 * D], bh_row[:, 0:2 * D], ALU.add).then_inc(rows_ready, 1)
                    nc.vector.tensor_copy(c_row[:, 2 * D:3 * D], bi_row[:, 2 * D:3 * D])
                    nc.vector.tensor_copy(c_row[:, 3 * D:4 * D], bh_row[:, 2 * D:3 * D]).then_inc(rows_ready, 1)
                    dve.wait_ge(rows_ready, 1)
                    nc.vector.tensor_copy(ones2[:, :], ones_f[:, :])
                    dve.wait_ge(rows_high, 1)
                    nc.vector.tensor_tensor(c_low[:, :], c_row[:, :], c_high[:, :], ALU.subtract).then_inc(rows_low, 1)
                    dve.wait_ge(edges_loaded, 64)
                    nc.vector.memset(tile_i[:, EC:EC + 2], 0)
                    nc.vector.tensor_scalar(tile_i[:, 0:EC], src_i[:, :], 7, None, ALU.logical_shift_right).then_inc(prep, 1)
                    nc.vector.tensor_scalar(pay_all[:, 0:EC], src_i[:, :], P - 1, 16, ALU.bitwise_and,
                                            ALU.logical_shift_left).then_inc(prep, 1)
                    dve.wait_ge(prep, 1)
                    nc.vector.tensor_copy(tile_f[:, :], tile_i[:, :])
                    dve.wait_ge(prep, 2)
                    nc.vector.tensor_tensor(pay_all[:, 0:EC], pay_all[:, 0:EC], dst_i[:, :], ALU.bitwise_or)
                    high = 0
                    for n, (_, target, col, _) in enumerate(banks_of):
                        if target is not None:
                            high += 1
                            dve.wait_ge(w_high, high)
                            nc.vector.tensor_tensor(flat(target[1])[:, col:col + 512], banks[n][:, :],
                                                    flat(target[0])[:, col:col + 512], ALU.subtract)

        xt2_done = sem("xt2_done")
        high2_done = sem("high2_done")
        low2_done = sem("low2_done")
        rowmm_done = sem("rowmm_done")
        row_evac = sem("row_evac")
        row_stored = [sem(f"row_stored{n}") for n in range(2)]
        onehot_ready = sem("onehot_ready")
        rank_mm = [sem(f"rank_mm{n}") for n in range(2)]
        rank_read = [sem(f"rank_read{n}") for n in range(2)]
        rank_int = sem("rank_int")
        index_ready = sem("index_ready")
        index_copied = sem("index_copied")
        scattered = [sem(f"scattered{n}") for n in range(2)]
        index_kept = sem("index_kept")
        counts_done = sem("counts_done")
        banks_marked = sem("banks_marked")
        b1_put = sem("b1_put")
        wc_done = sem("wc_done")
        wc_high = sem("wc_high")
        rounds_done = sem("rounds_done")
        with ExitStack() as tmp:
            def tb(name, shape, dt):
                return tmp.enter_context(nc.sbuf_tensor("sb_" + name, shape, dt))

            onehot = tb("onehot", [P, 3, 2, NW], F16)
            scratch = tb("scratch", [P, 2, NW], F16)
            rank = tb("rank", [P, 2, 2 * MP], F32)
            rank_i = tb("rank_i", [P, 2, 2 * MP], I32)
            index = tb("index", [P, 2, 2 * MP], I32)
            pay = tb("pay", [P, 2, 2 * MP], I32)
            rounds_f = tb("rounds_f", [P, 1], F32)
            rounds_t = tb("rounds_t", [P, 1], I32)
            xt_high = tb("xt_high", [P, 2, KC, P], F32R)
            xt_low = tb("xt_low", [P, 2, KC, P], F32R)
            rows = tb("rows", [P, 2, MT, D], F32)

            rank_bank = banks[0:2]
            xt_bank = banks[2:4]
            row_bank = banks[4:6]
            wc_bank = (banks[6], banks[7], banks[2])
            def macro_steps(eng, step):
                for c in range(MACROS_FIRST):
                    step(0, c)
                with eng.Fori(0, (MACROS - 1 - MACROS_FIRST - MACROS_UNROLL) // 2 + 1, MACROS_UNROLL // 2) as u:
                    for c in range(MACROS_FIRST, MACROS_FIRST + MACROS_UNROLL):
                        step(u, c)
                step(0, MACROS - 1)

            def tiles_of(c):
                return LAST_MT if c == MACROS - 1 else MT

            def pairs_of(c):
                return LAST_MP if c == MACROS - 1 else MP

            def node_rows(t, u, c):
                if c == MACROS - 1:
                    return t[c * MT * P:N, :].rearrange("(p q) d -> p q d", q=LAST_MT), TAIL_P, LAST_MT
                return t[bass.ds((2 * u + c) * (MT * P), MT * P), :].rearrange("(p q) d -> p q d", q=MT), P, MT

            with nc.Block() as block:
                @block.sync
                def _(sp):
                    def store(u, c):
                        rows_out, np_, nq = node_rows(xb_rows, u, c)
                        sp.wait_ge(row_evac, 2 * MT * u + (MT * c + tiles_of(c)))
                        sp.dma_start(rows_out, rows[0:np_, c % 2, 0:nq, :]).then_inc(row_stored[c % 2], 16)

                    def step(u, c):
                        if c >= 2:
                            rows_in, np_, nq = node_rows(x, u, c)
                            sp.wait_ge(xt2_done, 2 * MT * u + MT * (c - 1))
                            sp.dma_start(x2[0:np_, c % 2, 0:nq, :], rows_in).then_inc(x_in[c % 2], 16)
                            store(u, c - 2)

                    macro_steps(sp, step)
                    store(0, MACROS - 2)
                    store(0, MACROS - 1)
                    sp.wait_ge(row_stored[0], 16 * ((MACROS + 1) // 2))
                    sp.wait_ge(row_stored[1], 16 * (MACROS // 2))
                    sp.wait_ge(rows_placed, 64)

                @block.tensor
                def _(pe):
                    def transposes(u, c, q):
                        if q == 0:
                            pe.wait_ge(x_in[c % 2], 16 * u + 16 * (c // 2 + 1))
                        k = MT * c + q
                        if k >= 2:
                            pe.wait_ge(low2_done, 2 * MT * u + (k - 1))
                        for d in range(KC):
                            last = nc.tensor.transpose(xt_bank[q % 2][:, d * P:(d + 1) * P], x2[:, c % 2, q, d * P:(d + 1) * P], ident[:, :])
                        last.then_inc(xt2_done, 1)

                    def product(u, c, q):
                        k = MT * c + q
                        pe.wait_ge(low2_done, 2 * MT * u + (k + 1))
                        pe.wait_ge(b1_put, 2 * MT * u + (k + 1))
                        n = 0
                        for xt, w in ((xt_high, w1b[0]), (xt_high, w1b[1]), (xt_low, w1b[0])):
                            for d in range(KC):
                                last = nc.tensor.matmul(row_bank[q % 2][:, 0:D], xt[:, q % 2, d, :], w[:, d, :], start=False, stop=(n == 5),
                                                        skip_group_check=True)
                                n += 1
                        last.then_inc(rowmm_done, 1)

                    def count(bank, left, q, half, first=False, last=False):
                        return nc.tensor.matmul(rank_bank[bank][:, 0:NW], left[:, :], onehot[:, q % 3, half, :],
                                                start=first, stop=last, skip_group_check=True)

                    def ranks(u, c, q):
                        g = MP * c + q
                        first = g == 0
                        if not first:
                            pe.wait_ge(rank_read[0], 2 * MP * u + g)
                            count(0, rest, q - 1, 0)
                            count(0, ones16, q - 1, 1)
                        pe.wait_ge(onehot_ready, 2 * MP * u + (g + 1))
                        count(0, tri, q, 0, first, True).then_inc(rank_mm[0], 1)
                        if not first:
                            pe.wait_ge(rank_read[1], 2 * MP * u + g)
                            count(1, rest, q - 1, 1)
                        count(1, ones16, q, 0, first)
                        count(1, tri, q, 1, False, True).then_inc(rank_mm[1], 1)

                    def step(u, c):
                        for q in range(tiles_of(c)):
                            transposes(u, c, q)
                            if q < pairs_of(c):
                                ranks(u, c, q)
                            if c or q:
                                if q:
                                    product(u, c, q - 1)
                                else:
                                    product(u, c - 1, MT - 1)

                    for bank in row_bank:
                        nc.tensor.matmul(bank[:, 0:D], ones16[:, :], tiles16[:, 0:D], start=True, stop=True).then_inc(banks_marked, 1)
                    macro_steps(pe, step)
                    product(0, MACROS - 1, LAST_MT - 1)
                    pe.wait_ge(rank_read[0], PAIRS)
                    count(0, rest, LAST_MP - 1, 0)
                    count(0, ones16, LAST_MP - 1, 1, False, True).then_inc(counts_done, 1)
                    pe.wait_ge(late_loaded, 64)
                    for n, bank in enumerate(wc_bank):
                        if n == 2:
                            pe.wait_ge(low2_done, NT)
                        for half in range(2):
                            k, c = divmod(2 * n + half, 3)
                            for d in range(KC):
                                last = nc.tensor.matmul(bank[:, half * D:(half + 1) * D], w2_raw[:, d, k * P:(k + 1) * P],
                                                        wih_t[:, d, c * D:(c + 1) * D], start=(d == 0), stop=(d == KC - 1))
                        last.then_inc(wc_done, 1)

                @block.scalar
                def _(act):
                    def high(u, c, q):
                        k = MT * c + q
                        act.wait_ge(xt2_done, 2 * MT * u + (k + 1))
                        if k >= 2:
                            act.wait_ge(rowmm_done, 2 * MT * u + (k - 1))
                        nc.scalar.activation(xt_high[:, q % 2, :, :].rearrange("p k n -> p (k n)"), xt_bank[q % 2][:, 0:D], ACT.Copy).then_inc(high2_done, 1)

                    def put_b1(u, c, q):
                        k = MT * c + q
                        if k < 2:
                            act.wait_ge(banks_marked, k + 1)
                        else:
                            act.wait_ge(row_evac, 2 * MT * u + (k - 1))
                        nc.scalar.activation(row_bank[q % 2][:, 0:D], b1_wide[:, :], ACT.Copy).then_inc(b1_put, 1)

                    def evacuate(u, c, q):
                        k = MT * c + q
                        act.wait_ge(rowmm_done, 2 * MT * u + (k + 1))
                        if q == 0 and c >= 2:
                            act.wait_ge(row_stored[c % 2], 16 * u + 16 * (c // 2))
                        nc.scalar.activation(rows[:, c % 2, q, :], row_bank[q % 2][:, 0:D], ACT.Copy).then_inc(row_evac, 1)

                    def payload(u, c):
                        b = 2 * pairs_of(c)
                        if c >= 2:
                            act.wait_ge(scattered[c % 2], 32 * MP * u + 32 * MP * (c // 2))
                        nc.scalar.activation(pay[:, c % 2, 0:b], pay_all[:, bass.ds(4 * MP * u + 2 * MP * c, b)], ACT.Copy).then_inc(index_copied, 1)

                    def step(u, c):
                        for q in range(tiles_of(c)):
                            if q == 2:
                                payload(u, c)
                            high(u, c, q)
                            put_b1(u, c, q)
                            if c or q:
                                if q:
                                    evacuate(u, c, q - 1)
                                else:
                                    evacuate(u, c - 1, MT - 1)

                    act.wait_ge(b1_loaded, 16)
                    macro_steps(act, step)
                    evacuate(0, MACROS - 1, LAST_MT - 1)
                    for n, bank in enumerate(wc_bank):
                        act.wait_ge(wc_done, n + 1)
                        nc.scalar.activation(flat(wc[0])[:, n * 512:(n + 1) * 512], bank[:, :], ACT.Copy).then_inc(wc_high, 1)

                @block.vector
                def _(dve):
                    def onehots(u, c, q):
                        g = MP * c + q
                        if g >= 3:
                            dve.wait_ge(rank_mm[1], 2 * MP * u + (g - 1))
                        for half in range(2):
                            last = nc.vector.tensor_scalar(onehot[:, q % 3, half, :], tiles16[:, :],
                                                           tile_f[:, bass.ds(4 * MP * u + (2 * g + half), 1)], None, ALU.is_equal)
                        last.then_inc(onehot_ready, 1)

                    def read_ranks(u, c, q):
                        g = MP * c + q
                        for half in range(2):
                            dve.wait_ge(rank_mm[half], 2 * MP * u + (g + 1))
                            nc.vector.tensor_tensor_reduce(out=scratch[:, half, :], in0=rank_bank[half][:, 0:NW], in1=onehot[:, q, half, :],
                                                           scale=1.0, scalar=0.0, op0=ALU.mult, op1=ALU.add,
                                                           accum_out=rank[:, c % 2, 2 * q + half:2 * q + half + 1]).then_inc(rank_read[half], 1)

                    def low(u, c, q):
                        k = MT * c + q
                        dve.wait_ge(high2_done, 2 * MT * u + (k + 1))
                        nc.vector.tensor_tensor(xt_low[:, q % 2, :, :].rearrange("p k n -> p (k n)"), xt_bank[q % 2][:, 0:D],
                                                xt_high[:, q % 2, :, :].rearrange("p k n -> p (k n)"), ALU.subtract).then_inc(low2_done, 1)

                    def whole_ranks(u, c):
                        b = 2 * pairs_of(c)
                        dve.wait_ge(rank_read[1], 2 * MP * u + (MP * c + pairs_of(c)))
                        nc.vector.tensor_copy(rank_i[:, c % 2, 0:b], rank[:, c % 2, 0:b]).then_inc(rank_int, 1)

                    def indices(u, c):
                        b = 2 * pairs_of(c)
                        dve.wait_ge(rank_int, 2 * u + (c + 1))
                        if c >= 2:
                            dve.wait_ge(scattered[c % 2], 32 * MP * u + 32 * MP * (c // 2))
                            dve.wait_ge(index_kept, 2 * u + (c - 1))
                        nc.vector.scalar_tensor_tensor(out=index[:, c % 2, 0:b], in0=rank_i[:, c % 2, 0:b], scalar=ES,
                                                       in1=tile_i[:, bass.ds(4 * MP * u + 2 * MP * c, b)],
                                                       op0=ALU.logical_shift_left, op1=ALU.bitwise_or).then_inc(index_ready, 1)

                    def step(u, c):
                        for q in range(tiles_of(c)):
                            if q < pairs_of(c):
                                if q + 1 < pairs_of(c):
                                    onehots(u, c, q + 1)
                                elif c + 1 < MACROS:
                                    onehots(u, c + 1, 0)
                            low(u, c, q)
                            if q < pairs_of(c):
                                read_ranks(u, c, q)
                            if q == pairs_of(c) - 1:
                                whole_ranks(u, c)
                            if q == min(pairs_of(c), tiles_of(c) - 1):
                                indices(u, c)

                    onehots(0, 0, 0)
                    macro_steps(dve, step)
                    dve.wait_ge(counts_done, 1)
                    nc.vector.reduce_max(rounds_f[:, :], rank_bank[0][:, 0:NW], AX.X).then_inc(rounds_done, 1)
                    dve.wait_ge(rounds_done, 1)
                    nc.vector.tensor_scalar(rounds_t[:, :], rounds_f[:, :], float(P - 1), None, ALU.add).then_inc(rounds_done, 1)
                    dve.wait_ge(rounds_done, 2)
                    nc.vector.tensor_scalar(rounds_i[:, :], rounds_t[:, :], 7, None, ALU.logical_shift_right).then_inc(rounds_done, 1)
                    for n, bank in enumerate(wc_bank):
                        dve.wait_ge(wc_high, n + 1)
                        nc.vector.tensor_tensor(flat(wc[1])[:, n * 512:(n + 1) * 512], bank[:, :],
                                                flat(wc[0])[:, n * 512:(n + 1) * 512], ALU.subtract)

                @block.gpsimd
                def _(pool):
                    last_entry = pool.to_reg(FAST * ROUND - 1)
                    pool.wait_ge(table_cleared, 16)

                    def step(u, c):
                        b = 2 * pairs_of(c)
                        pool.wait_ge(index_ready, 2 * u + (c + 1))
                        pool.wait_ge(index_copied, 2 * u + (c + 1))
                        nc.gpsimd.tensor_copy(index_all[:, bass.ds(4 * MP * u + 2 * MP * c, b)], index[:, c % 2, 0:b]).then_inc(index_kept, 1)
                        for n in range(b):
                            pool.indirect_dma_start(table, bass.IndirectOffsetOnAxis(ap=index[:, c % 2, n:n + 1], axis=0),
                                                    pay[:, c % 2, n:n + 1], None, bounds_check=last_entry,
                                                    oob_is_err=False).then_inc(scattered[c % 2], 16)

                    macro_steps(pool, step)
                    pool.wait_ge(scattered[0], 32 * MP * (MACROS // 2))
                    pool.wait_ge(scattered[1], 32 * MP * (MACROS // 2 - 1) + 32 * LAST_MP)

        stage2.close()

        rounds_there = sem("rounds_there")
        free_made = sem("free_made")
        further_done = sem("further_done")
        again_copied = sem("again_copied")
        again_scattered = sem("again_scattered")
        b2w_done = sem("b2w_done")
        b2w_high_done = sem("b2w_high_done")
        m_free = sem("m_free")
        rounds = {}
        table_rows = table.rearrange("(q h) a -> q (h a)", h=TW)
        decoded = sem("decoded")
        fixed_made = sem("fixed_made")
        with ExitStack() as tmp:
            def tb(name, shape, dt):
                return tmp.enter_context(nc.sbuf_tensor("sb_" + name, shape, dt))

            xs = tb("xs", [P, XS, D], F32)
            slot = tb("slot", [P, 3, 2 * FAST], I32)
            got = tb("got", [P, 3, FAST * D], F32)
            sel16 = tb("sel16", [P, 3, FAST, P], F16)
            sel = tb("sel", [P, 3, FAST, P], F32R)
            sel_t = tb("sel_t", [P, 3, FAST * P], F32R)
            xh = tb("xh", [P, 2, KC, P], F32R)
            xl = tb("xl", [P, 2, KC, P], F32R)
            ah = tb("ah", [P, 2, D], F32R)
            al = tb("al", [P, 2, D], F32R)
            pre = tb("pre", [P, 2, FAST * D], F32)
            msg = tb("msg", [P, FAST, D], F32)
            msg_h = tb("msg_h", [P, 2, FAST, D + 2], F32R)
            msg_l = tb("msg_l", [P, 2, FAST, D], F32R)
            inv = tb("inv", [P, 2, 2], F32)
            mean = tb("mean", [P, 2, 3 * P], F32)
            mh = tb("mh", [P, 2, 3 * P], F32R)
            ml = tb("ml", [P, 2, 2 * P], F32R)
            trz = tb("trz", [P, 2, 2 * D], F32)
            u_sb = tb("u_sb", [P, 2, D], F32)
            cand_in = tb("cand_in", [P, 2, D], F32)
            cand = tb("cand", [P, 2, D], F32)
            diff = tb("diff", [P, 2, D], F32)
            xbeta = tb("xbeta", [P, 3, D], F32)
            zd = tb("zd", [P, 2, D], F32)
            xn = tb("xn", [P, 3, D], F32)
            stats = tb("stats", [P, 2, 6], F32)
            mv = tb("mv", [P, 2, 3, 2], F32)
            shift = tb("shift", [P, 3], F32)
            arg = tb("arg", [P, 2, 3], F32)
            minus_mean = tb("minus_mean", [P, 3], F32)
            rstd = tb("rstd", [P, 2, 3], F32)
            g_sb = tb("g_sb", [P, 2, D], F32)
            o_sb = tb("o_sb", [P, 3, D], F32)
            out_sb = tb("out_sb", [P, 3, D], F32)
            raw = tb("raw", [P, FAST, TW], I32)
            lanes_i = tb("lanes_i", [P, FAST, TW], I32)

            free = tb("free", [P, TW], I32)
            spare = tb("spare", [P, 2], F32)
            spare_v = tb("spare_v", [P, 1], F32)
            again = tb("again", [P, 2, 2], I32)
            more_i = tb("more_i", [1, 2, NW], I32)
            more_f = tb("more_f", [1, 3, NW], F32)
            further_i = tb("further_i", [1, 2, NW], I32)
            m_raw = tb("m_raw", [P, 1], I32)
            m_dst = tb("m_dst", [P, 1], I32)
            m_lane_i = tb("m_lane_i", [P, 1], I32)
            m_lane = tb("m_lane", [P, 1], F32)
            m_sel = tb("m_sel", [P, P], F32R)
            m_sel_t = tb("m_sel_t", [P, P], F32R)
            m_got = tb("m_got", [P, D], F32)
            m_pre = tb("m_pre", [P, D], F32)
            m_msg = tb("m_msg", [P, D], F32)
            m_high = tb("m_high", [P, D + 2], F32R)
            m_low = tb("m_low", [P, D], F32R)

            b_rz = banks[0:2]
            b_pre, b_sum, b_mean, b_n, b_a = banks[2:7]
            b_xt, b_selt, b_mselt = banks[7][:, 0:D], banks[7][:, D:D + FAST * P // 2].bitcast(F16), banks[7][:, D:D + P]

            with nc.Block() as block:
                @block.sync
                def _(sp):
                    for q in range(FAST):
                        sp.dma_start(raw[:, q, :], table_rows[q * P:(q + 1) * P, :]).then_inc(rounds_there, 16)
                    rounds["SP"] = sp.value_load(rounds_i[0:1, 0:1], min_val=0, max_val=ROUNDS)
                    with sp.If(rounds["SP"] > FAST):
                        sp.wait_ge(free_made, 1)
                        with sp.Fori(FAST, rounds["SP"]) as q:
                            sp.dma_start(table_rows[bass.ds(q * P, P), :], free[:, :]).then_inc(rounds_there, 16)

                @block.tensor
                def _(pe):
                    nc.tensor.transpose(banks[1][:, 0:P], ident[:, :], ident[:, :]).then_inc(m_free, 1)
                    for n, (a, z) in enumerate(((0, 2 * D), (2 * D, 3 * D))):
                        for d in range(KC):
                            last = nc.tensor.matmul(banks[2 + n][0:1, 0:z - a], b2_col[:, d:d + 1], wih_t[:, d, a:z],
                                                    start=(d == 0), stop=(d == KC - 1))
                        last.then_inc(b2w_done, 1)
                    rounds["PE"] = pe.value_load(rounds_i[0:1, 0:1], min_val=0, max_val=ROUNDS)

                @block.scalar
                def _(act):
                    for n, (a, z) in enumerate(((0, 2 * D), (2 * D, 3 * D))):
                        act.wait_ge(b2w_done, n + 1)
                        nc.scalar.activation(b2w_high[:, a:z], banks[2 + n][0:1, 0:z - a], ACT.Copy).then_inc(b2w_high_done, 1)
                    rounds["ACT"] = act.value_load(rounds_i[0:1, 0:1], min_val=0, max_val=ROUNDS)

                @block.gpsimd
                def _(pool):
                    nc.gpsimd.memset(msg_h[:, :, :, D:D + 2].bitcast(F32), 1.0)
                    nc.gpsimd.memset(m_high[:, D:D + 2].bitcast(F32), 1.0)
                    nc.gpsimd.memset(mean[:, :, 2 * P:3 * P], 0.0).then_inc(fixed_made, 1)
                    pool.wait_ge(fixed_made, 1)
                    nc.gpsimd.memset(mean[:, :, 2 * P + 2:2 * P + 4], 1.0)
                    rounds["POOL"] = pool.value_load(rounds_i[0:1, 0:1], min_val=0, max_val=ROUNDS)

                    def scatter_again(v, first):
                        if not first:
                            pool.wait_ge(again_scattered, v * 32)
                        nc.gpsimd.tensor_tensor(spare[:, 1:2], lane[:, 0:1], lane[:, 0:1], ALU.add)
                        nc.gpsimd.tensor_copy(again[:, 0, :], index_all[:, bass.ds(2 * v, 2)])
                        nc.gpsimd.tensor_copy(again[:, 1, :], pay_all[:, bass.ds(2 * v, 2)]).then_inc(again_copied, 1)
                        pool.wait_ge(again_copied, v + 1)
                        nc.gpsimd.tensor_tensor(spare[:, 0:1], lane[:, 0:1], lane[:, 0:1], ALU.add)
                        for n in range(2):
                            pool.indirect_dma_start(table, bass.IndirectOffsetOnAxis(ap=again[:, 0, n:n + 1], axis=0),
                                                    again[:, 1, n:n + 1], None).then_inc(again_scattered, 16)

                    with pool.If(rounds["POOL"] > FAST):
                        pool.wait_ge(rounds_there, rounds["POOL"] * 16)
                        scatter_again(0, True)
                        with pool.Fori(1, PAIRS) as v:
                            scatter_again(v, False)
                        pool.wait_ge(again_scattered, 32 * PAIRS)

                @block.vector
                def _(dve):
                    dve.wait_ge(rounds_there, 16 * FAST)
                    nc.vector.tensor_scalar(slots[:, 0:FAST, :], raw[:, :, :], 0xFFFF, None, ALU.bitwise_and)
                    nc.vector.tensor_scalar(lanes_i[:, :, :], raw[:, :, :], 16, None, ALU.logical_shift_right).then_inc(decoded, 1)
                    dve.wait_ge(decoded, 1)
                    nc.vector.tensor_copy(slots[:, FAST:2 * FAST, :].bitcast(F32), lanes_i[:, :, :]).then_inc(decoded, 1)
                    for n, (a, z) in enumerate(((0, 2 * D), (2 * D, 3 * D))):
                        dve.wait_ge(b2w_high_done, n + 1)
                        nc.vector.tensor_tensor(b2w_low[:, a:z], banks[2 + n][0:1, 0:z - a], b2w_high[:, a:z], ALU.subtract)
                    rounds["DVE"] = dve.value_load(rounds_i[0:1, 0:1], min_val=0, max_val=ROUNDS)
                    with dve.If(rounds["DVE"] > FAST):
                        nc.vector.memset(free[:, :], EMPTY).then_inc(free_made, 1)
                        nc.vector.tensor_scalar(more_i[:, 0, :], banks[0][0:1, 0:NW], float(P - 1), None, ALU.add).then_inc(further_done, 1)
                        dve.wait_ge(further_done, 1)
                        nc.vector.tensor_scalar(more_i[:, 1, :], more_i[:, 0, :], 7, None, ALU.logical_shift_right).then_inc(further_done, 1)
                        dve.wait_ge(further_done, 2)
                        nc.vector.tensor_scalar(more_f[:, 0, :], more_i[:, 1, :], float(FAST), float(FAST), ALU.max, ALU.subtract).then_inc(further_done, 1)
                        nc.vector.memset(more_f[:, 2, :], 0.0).then_inc(further_done, 1)
                        dve.wait_ge(further_done, 4)
                        nc.vector.tensor_copy(further_i[:, 0, :], more_f[:, 0, :])
                        nc.vector.tensor_tensor_scan(more_f[:, 1, :], more_f[:, 0, :], more_f[:, 2, :], 0.0, ALU.add, ALU.add).then_inc(further_done, 1)
                        dve.wait_ge(further_done, 5)
                        nc.vector.tensor_tensor(further_i[:, 1, :], more_f[:, 1, :], more_f[:, 0, :], ALU.subtract).then_inc(further_done, 1)

            names = ("slot_ready sel16_ready sel_ready selt_copied xt_done xh_done xl_done a_done a_ready "
                     "pre_done pre_ready sum_done inv_done mean_ready mt_done mh_done ml_done hn_done rz_done n_done "
                     "trz_done u_done cand_in_done cand_done diff_done xbeta_done zd_done xn_done stats_done mv_done "
                     "arg1_done arg2_done minus_done rstd1_done rstd2_done shift_done g_done o_done stats2_done mv2_done out_ready silu_f_done msg_l_done ah_done "
                     "m_split m_dst_done m_lane_done m_sel_done m_selt_done m_selt_copied m_spread m_added m_silu_h_done "
                     "m_silu_done m_low_done").split()
            S = {n: sem(n) for n in names}
            x_loaded = [sem(f"x_loaded{n}") for n in range(XS)]
            gathered = [sem(f"gathered{n}") for n in range(3)]
            out_stored = [sem(f"out_stored{n}") for n in range(3)]
            m_loaded = sem("m_loaded")
            m_gathered = sem("m_gathered")

            def run(eng, stages, lo, hi):
                def step(u, c):
                    for off, stage in stages:
                        if c + off >= 0 and (c >= LO and not isinstance(u, int) or c + off < NT):
                            stage(u, c + off)
                for c in range(lo, LO):
                    step(0, c)
                with eng.Fori(0, LOOPS) as u:
                    for c in range(LO, LO + XS):
                        step(u, c)
                for c in range(HI, hi):
                    step(0, c)

            def in_turn(eng, stages, further, summed=None):
                def tile(u, c):
                    for stage in stages:
                        if stage is not further:
                            stage(u, c)
                            continue
                        number = eng.value_load(further_i[0:1, 0, bass.ds(XS * u + c, 1)], min_val=0, max_val=ROUNDS - FAST)
                        before = eng.value_load(further_i[0:1, 1, bass.ds(XS * u + c, 1)], min_val=0, max_val=ROUNDS - FAST)
                        with eng.If(number > 0):
                            with eng.Fori(0, number) as e:
                                further(u, c, before + e, e)
                        if summed:
                            summed(before + number)

                for c in range(XS):
                    tile(0, c)
                with eng.Fori(0, (NT - XS) // XS) as u:
                    for c in range(XS, 2 * XS):
                        tile(u, c)
                for c in range(NT // XS * XS, NT):
                    tile(0, c)

            def rows_of(c):
                return LAST_ROWS if c == NT - 1 else P

            def tile_rows(t, u, c):
                return t[bass.ds((XS * u + c) * P, rows_of(c)), :]

            LOAD, STORE = 4, -5
            with nc.Block() as block:
                @block.sync
                def _(sp):
                    sp.dma_start(gi_bias[0:1, :].bitcast(F32), b2w_high[:, :].bitcast(F32)).then_inc(rows_placed, 16)
                    sp.dma_start(gi_bias[1:2, :].bitcast(F32), b2w_low[:, :].bitcast(F32)).then_inc(rows_placed, 16)

                    def load(u, c):
                        if c >= XS:
                            sp.wait_ge(S["diff_done"], XS * u + (c - XS + 1))
                            sp.wait_ge(S["xbeta_done"], XS * u + (c - XS + 1))
                        sp.dma_start(xs[0:rows_of(c), c % XS, :], tile_rows(x, u, c)).then_inc(x_loaded[c % XS], 16)

                    def store(u, c):
                        sp.wait_ge(S["out_ready"], XS * u + (c + 1))
                        sp.dma_start(tile_rows(out, u, c), out_sb[0:rows_of(c), c % 3, :]).then_inc(out_stored[c % 3], 16)

                    def further(u, c, q, e):
                        sp.wait_ge(m_free, q + 1)
                        with nc.allow_non_contiguous_dma(reason="a column of the table"):
                            sp.dma_start(m_raw[:, :], table_rows[bass.ds((e + FAST) * P, P), bass.ds(XS * u + c, 1)]).then_inc(m_loaded, 16)

                    with sp.If(rounds["SP"] <= FAST):
                        run(sp, ((LOAD, load), (STORE, store)), -LOAD, NT - STORE)
                    with sp.Else():
                        in_turn(sp, (load, further, store), further)
                    for n in range(3):
                        sp.wait_ge(out_stored[n], 16 * len(range(n, NT, 3)))

                @block.tensor
                def _(pe):
                    def transposes(u, c):
                        pe.wait_ge(x_loaded[c % XS], 16 * u + 16 * (c // XS + 1))
                        pe.wait_ge(S["sel16_ready"], XS * u + (c + 1))
                        if c >= 1:
                            pe.wait_ge(S["xl_done"], XS * u + c)
                            pe.wait_ge(S["selt_copied"], XS * u + c)
                        for k in range(KC):
                            nc.tensor.transpose(b_xt[:, k * P:(k + 1) * P], xs[:, c % XS, k * P:(k + 1) * P], ident[:, :])
                        for r in range(FAST):
                            last = nc.tensor.transpose(b_selt[:, r * P:(r + 1) * P], sel16[:, c % 3, r, :], ident16[:, :])
                        last.then_inc(S["xt_done"], 1)

                    def split_product(bank, high, low, weight, a, z, first, last):
                        n = 0
                        for left, right in ((high, weight[0]), (high, weight[1]), (low, weight[0])):
                            for k in range(KC):
                                mm = nc.tensor.matmul(bank, left(k), right[:, k, a:z], start=first and n == 0, stop=last and n == 5)
                                n += 1
                        return mm

                    def x_parts(c):
                        return (lambda k: xh[:, c % 2, k, :]), (lambda k: xl[:, c % 2, k, :])

                    def mean_parts(c):
                        return ((lambda k: mh[:, c % 2, k * P:(k + 1) * P]), (lambda k: ml[:, c % 2, k * P:(k + 1) * P]))

                    def source_product(u, c):
                        pe.wait_ge(S["xl_done"], XS * u + (c + 1))
                        if c >= 1:
                            pe.wait_ge(S["a_ready"], XS * u + c)
                        split_product(b_a[:, 0:D], *x_parts(c), w1a, 0, D, True, True).then_inc(S["a_done"], 1)

                    def hidden_gates(u, c):
                        if c >= 2:
                            pe.wait_ge(S["trz_done"], XS * u + (c - 1))
                        split_product(b_rz[c % 2][:, :], *x_parts(c), whh, 0, 2 * D, True, False)

                    def hidden_candidate(u, c):
                        if c >= 1:
                            pe.wait_ge(S["cand_in_done"], XS * u + c)
                        nc.tensor.matmul(b_n[:, D:2 * D], ones2[:, :], hn_bias[:, :], start=True, stop=False)
                        split_product(b_n[:, D:2 * D], *x_parts(c), whh, 2 * D, 3 * D, False, True).then_inc(S["hn_done"], 1)

                    def spread_sources(u, c):
                        pe.wait_ge(S["a_ready"], XS * u + (c + 1))
                        pe.wait_ge(S["selt_copied"], XS * u + (c + 1))
                        if c >= 1:
                            pe.wait_ge(S["pre_ready"], XS * u + c)
                        for r in range(FAST):
                            nc.tensor.matmul(b_pre[:, r * D:(r + 1) * D], sel_t[:, c % 3, r * P:(r + 1) * P], ah[:, c % 2, :], start=True, stop=False)
                            last = nc.tensor.matmul(b_pre[:, r * D:(r + 1) * D], sel_t[:, c % 3, r * P:(r + 1) * P], al[:, c % 2, :], start=False, stop=True)
                        last.then_inc(S["pre_done"], 1)

                    def sum_messages(u, c):
                        pe.wait_ge(S["sel_ready"], XS * u + (c + 1))
                        pe.wait_ge(S["msg_l_done"], XS * u + (c + 1))
                        if c >= 1:
                            pe.wait_ge(S["mean_ready"], XS * u + c)
                        for r in range(FAST):
                            nc.tensor.matmul(b_sum[:, 0:D + 2], sel[:, c % 3, r, :], msg_h[:, c % 2, r, :], start=(r == 0), stop=False)
                            last = nc.tensor.matmul(b_sum[:, 0:D], sel[:, c % 3, r, :], msg_l[:, c % 2, r, :], start=False, stop=(r == FAST - 1))
                        last.then_inc(S["sum_done"], 1)

                    def transpose_mean(u, c):
                        pe.wait_ge(S["mean_ready"], XS * u + (c + 1))
                        if c >= 1:
                            pe.wait_ge(S["ml_done"], XS * u + c)
                        for k in range(3):
                            last = nc.tensor.transpose(b_mean[:, k * P:(k + 1) * P], mean[:, c % 2, k * P:(k + 1) * P], ident[:, :])
                        last.then_inc(S["mt_done"], 1)

                    def input_gates(u, c):
                        pe.wait_ge(S["ml_done"], XS * u + (c + 1))
                        bias_rows = mh[0:4, c % 2, 2 * P:3 * P]
                        nc.tensor.matmul(b_rz[c % 2][:, :], bias_rows, gi_bias[:, 0:2 * D], start=False, stop=False)
                        split_product(b_rz[c % 2][:, :], *mean_parts(c), wc, 0, 2 * D, False, True).then_inc(S["rz_done"], 1)
                        nc.tensor.matmul(b_n[:, 0:D], bias_rows, gi_bias[:, 2 * D:3 * D], start=True, stop=False)
                        split_product(b_n[:, 0:D], *mean_parts(c), wc, 2 * D, 3 * D, False, True).then_inc(S["n_done"], 1)

                    def further(u, c, q, e):
                        pe.wait_ge(S["m_sel_done"], q + 1)
                        nc.tensor.transpose(b_mselt, m_sel[:, :].bitcast(F32), ident[:, :]).then_inc(S["m_selt_done"], 1)
                        pe.wait_ge(S["m_selt_copied"], q + 1)
                        nc.tensor.matmul(b_pre[:, 0:D], m_sel_t[:, :], ah[:, c % 2, :], start=True, stop=False)
                        nc.tensor.matmul(b_pre[:, 0:D], m_sel_t[:, :], al[:, c % 2, :], start=False, stop=True).then_inc(S["m_spread"], 1)
                        pe.wait_ge(S["m_low_done"], q + 1)
                        nc.tensor.matmul(b_sum[:, 0:D + 2], m_sel[:, :], m_high[:, :], start=False, stop=False, skip_group_check=True)
                        nc.tensor.matmul(b_sum[:, 0:D], m_sel[:, :], m_low[:, :], start=False, stop=True, skip_group_check=True).then_inc(m_free, 1)

                    pe.wait_ge(rows_placed, 96)
                    with pe.If(rounds["PE"] <= FAST):
                        run(pe, ((0, spread_sources), (-1, transpose_mean), (0, hidden_gates), (-1, input_gates), (1, source_product), (0, sum_messages),
                                 (2, transposes), (0, hidden_candidate)), -2, NT + 1)
                    with pe.Else():
                        in_turn(pe, (transposes, source_product, spread_sources, hidden_gates, sum_messages, further,
                                     transpose_mean, hidden_candidate, input_gates), further)

                @block.scalar
                def _(act):
                    def mean_high(u, c):
                        act.wait_ge(S["mt_done"], XS * u + (c + 1))
                        if c >= 2:
                            act.wait_ge(S["n_done"], XS * u + (c - 1))
                        nc.scalar.activation(mh[:, c % 2, :], b_mean[:, 0:3 * P], ACT.Copy).then_inc(S["mh_done"], 1)

                    def x_high(u, c):
                        act.wait_ge(S["xt_done"], XS * u + (c + 1))
                        if c >= 2:
                            act.wait_ge(S["hn_done"], XS * u + (c - 1))
                        nc.scalar.activation(xh[:, c % 2, :, :].rearrange("p k n -> p (k n)"), b_xt, ACT.Copy).then_inc(S["xh_done"], 1)

                    def silu(u, c):
                        act.wait_ge(S["pre_ready"], XS * u + (c + 1))
                        if c >= 2:
                            act.wait_ge(S["sum_done"], XS * u + (c - 1))
                        rows_of_pre = pre[:, c % 2, :].rearrange("p (r d) -> p r d", r=FAST)
                        nc.scalar.activation(msg_h[:, c % 2, :, 0:D], rows_of_pre, ACT.Silu)
                        if c >= 1:
                            act.wait_ge(S["msg_l_done"], XS * u + c)
                        nc.scalar.activation(msg[:, :, :], rows_of_pre, ACT.Silu).then_inc(S["silu_f_done"], 1)

                    def gates(u, c):
                        act.wait_ge(S["rz_done"], XS * u + (c + 1))
                        if c >= 2:
                            act.wait_ge(S["xn_done"], XS * u + (c - 1))
                        nc.scalar.activation(trz[:, c % 2, :], b_rz[c % 2][:, :], ACT.Tanh, scale=0.5).then_inc(S["trz_done"], 1)

                    def widen_sel(u, c):
                        act.wait_ge(S["sel16_ready"], XS * u + (c + 1))
                        if c >= 3:
                            act.wait_ge(S["sum_done"], XS * u + (c - 2))
                        nc.scalar.activation(sel[:, c % 3, :, :], sel16[:, c % 3, :, :], ACT.Copy).then_inc(S["sel_ready"], 1)

                    def copy_sel_t(u, c):
                        act.wait_ge(S["xt_done"], XS * u + (c + 1))
                        if c >= 3:
                            act.wait_ge(S["pre_done"], XS * u + (c - 2))
                        nc.scalar.activation(sel_t[:, c % 3, :], b_selt, ACT.Copy).then_inc(S["selt_copied"], 1)

                    def candidate(u, c):
                        act.wait_ge(S["cand_in_done"], XS * u + (c + 1))
                        if c >= 2:
                            act.wait_ge(S["xn_done"], XS * u + (c - 1))
                        nc.scalar.activation(cand[:, c % 2, :], cand_in[:, c % 2, :], ACT.Tanh).then_inc(S["cand_done"], 1)

                    def source_high(u, c):
                        act.wait_ge(S["a_done"], XS * u + (c + 1))
                        if c >= 2:
                            act.wait_ge(S["pre_done"], XS * u + (c - 1))
                        nc.scalar.activation(ah[:, c % 2, :], b_a[:, 0:D], ACT.Copy).then_inc(S["ah_done"], 1)

                    def scale_sum(u, c):
                        act.wait_ge(S["inv_done"], 2 * XS * u + (2 * c + 2))
                        nc.scalar.activation(mean[:, c % 2, 0:D], b_sum[:, 0:D], ACT.Copy, scale=inv[:, 1, c % 2:c % 2 + 1]).then_inc(S["mean_ready"], 1)

                    def second_norm(u, c):
                        act.wait_ge(S["shift_done"], XS * u + (c + 1))
                        if c >= 3:
                            act.wait_ge(out_stored[c % 3], 32 * u + 16 * (c // 3))
                        nc.scalar.activation(out_sb[:, c % 3, :], o_sb[:, c % 3, :], ACT.Identity, bias=shift[:, c % 3:c % 3 + 1],
                                             scale=rstd[:, 1, c % 3:c % 3 + 1]).then_inc(S["out_ready"], 1)

                    def further(u, c, q, e):
                        act.wait_ge(S["m_selt_done"], q + 1)
                        nc.scalar.activation(m_sel_t[:, :], b_mselt, ACT.Copy).then_inc(S["m_selt_copied"], 1)
                        act.wait_ge(S["m_added"], q + 1)
                        nc.scalar.activation(m_high[:, 0:D], m_pre[:, :], ACT.Silu).then_inc(S["m_silu_h_done"], 1)
                        nc.scalar.activation(m_msg[:, :], m_pre[:, :], ACT.Silu).then_inc(S["m_silu_done"], 1)

                    with act.If(rounds["ACT"] <= FAST):
                        run(act, ((-1, mean_high), (1, x_high), (1, copy_sel_t), (0, silu), (-5, second_norm), (2, widen_sel), (-1, gates),
                                  (1, source_high), (-1, candidate), (0, scale_sum)), -2, NT + 5)
                    with act.Else():
                        in_turn(act, (widen_sel, x_high, copy_sel_t, source_high, silu, further, scale_sum, mean_high, gates, candidate,
                                      second_norm), further)

                @block.vector
                def _(dve):
                    def mean_low(u, c):
                        dve.wait_ge(S["mh_done"], XS * u + (c + 1))
                        nc.vector.tensor_tensor(ml[:, c % 2, :], b_mean[:, 0:2 * P], mh[:, c % 2, 0:2 * P], ALU.subtract).then_inc(S["ml_done"], 1)

                    def x_low(u, c):
                        dve.wait_ge(S["xh_done"], XS * u + (c + 1))
                        dve.wait_ge(S["selt_copied"], XS * u + (c + 1))
                        nc.vector.tensor_tensor(xl[:, c % 2, :, :].rearrange("p k n -> p (k n)"), b_xt,
                                                xh[:, c % 2, :, :].rearrange("p k n -> p (k n)"), ALU.subtract).then_inc(S["xl_done"], 1)

                    def add_destinations(u, c):
                        dve.wait_ge(S["pre_done"], XS * u + (c + 1))
                        dve.wait_ge(gathered[c % 3], 64 * u + 32 * (c // 3 + 1))
                        if c >= 2:
                            dve.wait_ge(S["silu_f_done"], XS * u + (c - 1))
                        nc.vector.tensor_tensor(pre[:, c % 2, :], b_pre[:, :], got[:, c % 3, :], ALU.add).then_inc(S["pre_ready"], 1)

                    def select(u, c):
                        dve.wait_ge(S["slot_ready"], XS * u + (c + 1))
                        if c >= 3:
                            dve.wait_ge(S["xt_done"], XS * u + (c - 2))
                            dve.wait_ge(S["sel_ready"], XS * u + (c - 2))
                        for r in range(FAST):
                            last = nc.vector.tensor_scalar(sel16[:, c % 3, r, :], lane16[:, :], slot[:, c % 3, FAST + r:FAST + r + 1].bitcast(F32),
                                                           None, ALU.is_equal)
                        last.then_inc(S["sel16_ready"], 1)

                    def reset_gate(u, c):
                        dve.wait_ge(S["trz_done"], XS * u + (c + 1))
                        dve.wait_ge(S["n_done"], XS * u + (c + 1))
                        nc.vector.scalar_tensor_tensor(out=u_sb[:, c % 2, :], in0=trz[:, c % 2, 0:D], scalar=1.0, in1=b_n[:, D:2 * D],
                                                       op0=ALU.add, op1=ALU.mult).then_inc(S["u_done"], 1)

                    def candidate_input(u, c):
                        dve.wait_ge(S["u_done"], XS * u + (c + 1))
                        if c >= 2:
                            dve.wait_ge(S["cand_done"], XS * u + (c - 1))
                        nc.vector.scalar_tensor_tensor(out=cand_in[:, c % 2, :], in0=u_sb[:, c % 2, :], scalar=0.5, in1=b_n[:, 0:D],
                                                       op0=ALU.mult, op1=ALU.add).then_inc(S["cand_in_done"], 1)

                    def source_low(u, c):
                        dve.wait_ge(S["ah_done"], XS * u + (c + 1))
                        nc.vector.tensor_tensor(al[:, c % 2, :], b_a[:, 0:D], ah[:, c % 2, :].bitcast(F32), ALU.subtract).then_inc(S["a_ready"], 1)

                    def gated_difference(u, c):
                        dve.wait_ge(S["diff_done"], XS * u + (c + 1))
                        nc.vector.scalar_tensor_tensor(out=zd[:, c % 2, :], in0=trz[:, c % 2, D:2 * D], scalar=1.0, in1=diff[:, c % 2, :],
                                                       op0=ALU.add, op1=ALU.mult).then_inc(S["zd_done"], 1)

                    def new_state(u, c):
                        dve.wait_ge(S["zd_done"], XS * u + (c + 1))
                        nc.vector.scalar_tensor_tensor(out=xn[:, c % 3, :], in0=zd[:, c % 2, :], scalar=0.5, in1=cand[:, c % 2, :],
                                                       op0=ALU.mult, op1=ALU.add).then_inc(S["xn_done"], 1)

                    def state_stats(u, c):
                        dve.wait_ge(S["xn_done"], XS * u + (c + 1))
                        nc.vector.bn_stats(stats[:, 0, :], xn[:, c % 3, :]).then_inc(S["stats_done"], 1)

                    def state_stats_there(u, c):
                        dve.wait_ge(S["stats_done"], XS * u + (c + 1))

                    def state_moments(u, c):
                        nc.vector.bn_aggr(mv[:, 0, c % 3, :], stats[:, 0, :]).then_inc(S["mv_done"], 1)

                    def number(u, c):
                        dve.wait_ge(S["sum_done"], XS * u + (c + 1))
                        if c >= 2:
                            dve.wait_ge(S["mt_done"], XS * u + (c - 1))
                        nc.vector.tensor_scalar(mean[:, c % 2, 2 * P:2 * P + 2], b_sum[:, D:D + 2], 1.0, None, ALU.min)
                        nc.vector.tensor_scalar(inv[:, 0, c % 2:c % 2 + 1], b_sum[:, D:D + 1], 1e-8, None, ALU.add).then_inc(S["inv_done"], 1)

                    def inverse(u, c):
                        dve.wait_ge(S["inv_done"], 2 * XS * u + (2 * c + 1))
                        nc.vector.reciprocal(inv[:, 1, c % 2:c % 2 + 1], inv[:, 0, c % 2:c % 2 + 1]).then_inc(S["inv_done"], 1)

                    def norm_gamma(u, c):
                        dve.wait_ge(S["rstd1_done"], XS * u + (c + 1))
                        nc.vector.scalar_tensor_tensor(out=g_sb[:, c % 2, :], in0=xn[:, c % 3, :], scalar=mv[:, 0, c % 3, 0:1], in1=gamma_b[:, :],
                                                       op0=ALU.subtract, op1=ALU.mult).then_inc(S["g_done"], 1)

                    def add_beta(u, c):
                        dve.wait_ge(x_loaded[c % XS], 16 * u + 16 * (c // XS + 1))
                        if c >= 3:
                            dve.wait_ge(S["o_done"], XS * u + (c - 2))
                        nc.vector.tensor_tensor(xbeta[:, c % 3, :], xs[:, c % XS, :], beta_b[:, :], ALU.add).then_inc(S["xbeta_done"], 1)

                    def residual(u, c):
                        dve.wait_ge(S["g_done"], XS * u + (c + 1))
                        dve.wait_ge(S["xbeta_done"], XS * u + (c + 1))
                        if c >= 3:
                            dve.wait_ge(S["out_ready"], XS * u + (c - 2))
                        nc.vector.scalar_tensor_tensor(out=o_sb[:, c % 3, :], in0=g_sb[:, c % 2, :], scalar=rstd[:, 0, c % 3:c % 3 + 1], in1=xbeta[:, c % 3, :],
                                                       op0=ALU.mult, op1=ALU.add).then_inc(S["o_done"], 1)

                    def residual_stats(u, c):
                        dve.wait_ge(S["o_done"], XS * u + (c + 1))
                        nc.vector.bn_stats(stats[:, 1, :], o_sb[:, c % 3, :]).then_inc(S["stats2_done"], 1)

                    def residual_stats_there(u, c):
                        dve.wait_ge(S["stats2_done"], XS * u + (c + 1))

                    def residual_moments(u, c):
                        nc.vector.bn_aggr(mv[:, 1, c % 3, :], stats[:, 1, :]).then_inc(S["mv2_done"], 1)

                    def apart(u, c):
                        nc.vector.memset(spare_v[:, :], 0.0)

                    def further(u, c, q, e):
                        dve.wait_ge(m_free, q + 1)
                        dve.wait_ge(m_loaded, q * 16 + 16)
                        nc.vector.tensor_scalar(m_dst[:, :], m_raw[:, :], 0xFFFF, None, ALU.bitwise_and).then_inc(S["m_dst_done"], 1)
                        nc.vector.tensor_scalar(m_lane_i[:, :], m_raw[:, :], 16, None, ALU.logical_shift_right).then_inc(S["m_split"], 1)
                        dve.wait_ge(S["m_split"], q + 1)
                        nc.vector.tensor_copy(m_lane[:, :], m_lane_i[:, :]).then_inc(S["m_lane_done"], 1)
                        dve.wait_ge(S["m_lane_done"], q + 1)
                        nc.vector.tensor_scalar(m_sel[:, :], lane[:, :], m_lane[:, :], None, ALU.is_equal).then_inc(S["m_sel_done"], 1)
                        dve.wait_ge(S["m_spread"], q + 1)
                        dve.wait_ge(m_gathered, q * 16 + 16)
                        nc.vector.tensor_tensor(m_pre[:, :], b_pre[:, 0:D], m_got[:, :], ALU.add).then_inc(S["m_added"], 1)

                    def summed(q):
                        dve.wait_ge(m_free, q + 1)

                    with dve.If(rounds["DVE"] <= FAST):
                        run(dve, ((0, add_destinations), (-1, mean_low), (-4, residual_stats), (-4, residual_stats_there),
                                  (-2, gated_difference), (-4, residual_moments), (2, select), (-2, new_state), (1, x_low),
                                  (-2, state_stats), (-2, state_stats_there), (-3, norm_gamma), (-2, state_moments),
                                  (-1, reset_gate), (-1, candidate_input), (0, number), (1, source_low), (0, inverse),
                                  (-1, add_beta), (-3, residual)), -2, NT + 4)
                    with dve.Else():
                        in_turn(dve, (select, x_low, source_low, add_destinations, further, number, inverse, mean_low, reset_gate,
                                      candidate_input, gated_difference, new_state, state_stats, state_stats_there, apart, state_moments,
                                      norm_gamma, add_beta, residual, residual_stats, residual_stats_there, apart, residual_moments),
                                further, summed)

                @block.gpsimd
                def _(pool):
                    def fetch_slot(u, c):
                        if c >= 3:
                            pool.wait_ge(S["sel16_ready"], XS * u + (c - 2))
                            pool.wait_ge(S["pre_ready"], XS * u + (c - 2))
                        nc.gpsimd.tensor_copy(slot[:, c % 3, :], slots[:, :, bass.ds(XS * u + c, 1)].rearrange("p r a -> p (r a)")).then_inc(S["slot_ready"], 1)

                    def slot_there(u, c):
                        pool.wait_ge(S["slot_ready"], XS * u + (c + 1))

                    def gather(u, c):
                        for r in range(FAST):
                            pool.indirect_dma_start(got[:, c % 3, r * D:(r + 1) * D], None, xb_rows,
                                                    bass.IndirectOffsetOnAxis(ap=slot[:, c % 3, r:r + 1], axis=0)).then_inc(gathered[c % 3], 16)

                    def differ(u, c):
                        pool.wait_ge(S["cand_done"], XS * u + (c + 1))
                        if c >= 2:
                            pool.wait_ge(S["zd_done"], XS * u + (c - 1))
                        nc.gpsimd.tensor_tensor(diff[:, c % 2, :], xs[:, c % XS, :], cand[:, c % 2, :], ALU.subtract).then_inc(S["diff_done"], 1)

                    def message_low(u, c):
                        pool.wait_ge(S["silu_f_done"], XS * u + (c + 1))
                        if c >= 2:
                            pool.wait_ge(S["sum_done"], XS * u + (c - 1))
                        nc.gpsimd.tensor_tensor(msg_l[:, c % 2, :, :], msg[:, :, :], msg_h[:, c % 2, :, 0:D].bitcast(F32), ALU.subtract).then_inc(S["msg_l_done"], 1)

                    def argument(u, c, norm, there, done):
                        pool.wait_ge(there, XS * u + (c + 1))
                        nc.gpsimd.tensor_tensor(arg[:, norm, c % 3:c % 3 + 1], mv[:, norm, c % 3, 1:2], columns[:, 1:2], ALU.add).then_inc(done, 1)

                    def root(u, c, norm, there, done):
                        pool.wait_ge(there, XS * u + (c + 1))
                        nc.gpsimd.tensor_tensor(rstd[:, norm, c % 3:c % 3 + 1], arg[:, norm, c % 3:c % 3 + 1], columns[:, 0:1], ALU.pow).then_inc(done, 1)

                    def state_argument(u, c):
                        argument(u, c, 0, S["mv_done"], S["arg1_done"])

                    def state_root(u, c):
                        root(u, c, 0, S["arg1_done"], S["rstd1_done"])

                    def residual_argument(u, c):
                        argument(u, c, 1, S["mv2_done"], S["arg2_done"])
                        nc.gpsimd.tensor_tensor(minus_mean[:, c % 3:c % 3 + 1], mv[:, 1, c % 3, 0:1], columns[:, 2:3], ALU.mult).then_inc(S["minus_done"], 1)

                    def residual_root(u, c):
                        root(u, c, 1, S["arg2_done"], S["rstd2_done"])

                    def shift_row(u, c):
                        pool.wait_ge(S["minus_done"], XS * u + (c + 1))
                        pool.wait_ge(S["rstd2_done"], XS * u + (c + 1))
                        nc.gpsimd.tensor_tensor(shift[:, c % 3:c % 3 + 1], minus_mean[:, c % 3:c % 3 + 1], rstd[:, 1, c % 3:c % 3 + 1], ALU.mult).then_inc(S["shift_done"], 1)

                    def apart(u, c):
                        nc.gpsimd.tensor_tensor(spare[:, 1:2], lane[:, 0:1], lane[:, 0:1], ALU.add)

                    def further(u, c, q, e):
                        pool.wait_ge(S["m_dst_done"], q + 1)
                        nc.gpsimd.tensor_tensor(spare[:, 0:1], lane[:, 0:1], lane[:, 0:1], ALU.add)
                        pool.indirect_dma_start(m_got[:, :], None, xb_rows,
                                                bass.IndirectOffsetOnAxis(ap=m_dst[:, :], axis=0)).then_inc(m_gathered, 16)
                        pool.wait_ge(S["m_silu_h_done"], q + 1)
                        pool.wait_ge(S["m_silu_done"], q + 1)
                        nc.gpsimd.tensor_tensor(m_low[:, :], m_msg[:, :], m_high[:, 0:D].bitcast(F32), ALU.subtract).then_inc(S["m_low_done"], 1)

                    with pool.If(rounds["POOL"] <= FAST):
                        run(pool, ((2, slot_there), (-5, shift_row), (2, gather), (0, message_low), (-4, residual_argument),
                                   (-4, residual_root), (-2, state_argument), (-2, state_root), (-1, differ), (3, fetch_slot)),
                            -3, NT + 5)
                    with pool.Else():
                        in_turn(pool, (fetch_slot, slot_there, apart, gather, message_low, further, differ,
                                       state_argument, state_root, residual_argument, residual_root, shift_row), further)


_INS = ['x', 'src', 'dst', 'L0_gnn_W1', 'L0_gnn_b1', 'L0_gnn_W2', 'L0_gnn_b2', 'L0_gnn_w_ih', 'L0_gnn_w_hh',
        'L0_gnn_b_ih', 'L0_gnn_b_hh', 'L0_gnn_gamma', 'L0_gnn_beta']


def kernel(**inputs):
    import numpy as _np
    import concourse.bacc as _bacc
    from concourse import mybir as _mybir
    from concourse.bass_utils import run_bass_kernel_spmd as _run

    nc = _bacc.Bacc("TRN2", target_bir_lowering=False, num_devices=1)
    arrays, args = {}, []
    for name in _INS:
        a = _np.ascontiguousarray(inputs[name])
        arrays[f"in_{name}_dram"] = a
        args.append(nc.dram_tensor(f"in_{name}_dram", a.shape, _mybir.dt.from_np(a.dtype), kind="ExternalInput").ap())
    out = nc.dram_tensor("out_0_dram", (N, D), F32, kind="ExternalOutput").ap()
    build(nc, *args, out)
    r = _run(nc, [arrays], core_ids=[0])
    return r.results[0]["out_0_dram"]
```
